# Optimizing a Trainium2 kernel written in Bass

```python
import numpy as np
import jax
import jax.numpy as jnp

def _softmax(x, axis=-1):
    return jax.nn.softmax(x, axis=axis)

def _gelu(x):
    return jax.nn.gelu(x, approximate=True)

def _silu(x):
    return jax.nn.silu(x)

def _sigmoid(x):
    return jax.nn.sigmoid(x)

def _layernorm(x, axis=-1, eps=1e-05):
    m = jnp.mean(x, axis=axis, keepdims=True)
    v = jnp.var(x, axis=axis, keepdims=True)
    return (x - m) / jnp.sqrt(v + eps)

def _scatter_add(tgt, idx, src, axis=0):
    return tgt.at[idx].add(src)

def _segment_sum(src, seg, n):
    return jax.ops.segment_sum(src, seg, n)
kernel_name = 'mk_decoder_postln_d1_seqx_r4_73246c'

def setup_inputs(seed: int=0):
    np.random.seed(seed)
    _w = jnp.asarray

    def _rec_inputs():
        import jax
        import jax.numpy as jnp
        _rk = jax.random.key(seed)
        x = -0.0003929 + 0.9999 * jax.random.normal(jax.random.fold_in(_rk, 1), (4, 1024, 256), jnp.float32)
        _lenS = 1024 - jax.random.randint(jax.random.fold_in(_rk, 7), (4,), 0, max(1, 1024 // 4) + 1, jnp.int32)
        _lenS2 = 77 - jax.random.randint(jax.random.fold_in(_rk, 8), (4,), 0, max(1, 77 // 4) + 1, jnp.int32)
        _ctx_1024P = jax.random.normal(jax.random.fold_in(_rk, 11), (4, 16, 256), jnp.float32)
        _ctx_1024c = jax.random.dirichlet(jax.random.fold_in(_rk, 511), 0.3 * jnp.ones((16,), jnp.float32), (4, 77))
        _ctx_1024t = jnp.einsum('bsk,bkd->bsd', _ctx_1024c, _ctx_1024P)
        _ctx_1024t = _ctx_1024t * jax.lax.rsqrt(jnp.mean(jnp.square(_ctx_1024t)) + 1e-12) * 0.953939
        ctx_1024 = -0.000514642 + 1.00011 * (_ctx_1024t + 0.3 * jax.random.normal(jax.random.fold_in(_rk, 611), (4, 77, 256), jnp.float32))
        _validS = jnp.arange(1024)[None, :] < _lenS[:, None]
        _validS2 = jnp.arange(77)[None, :] < _lenS2[:, None]
        _causal = jnp.tril(jnp.ones((1024, 1024), dtype=bool))
        mask_BxS2_bk0 = jnp.logical_not(jnp.broadcast_to(_validS2[:, :], (4, 77)))
        return (x, ctx_1024, mask_BxS2_bk0)
    x, ctx_1024, mask_BxS2_bk0 = _rec_inputs()

    def _L0_attn_setup():
        import jax, jax.numpy as jnp
        import numpy as np
        H_HEADS = 16
        STATE_N = 64

        def _mamba2_forward(inp, W_logA, b_logA, W_XBC, b_XBC, W_gate, b_gate, W_out, b_out):
            B, T, D = inp.shape
            H, N = (H_HEADS, STATE_N)
            ch = D // H
            x = inp.reshape(B, T, H, ch)
            logA = jnp.einsum('hoc,bthc->btho', W_logA, x)[..., 0] + b_logA[:, 0]
            XBC = jax.nn.silu(jnp.einsum('hoc,bthc->btho', W_XBC, x) + b_XBC)
            X = XBC[..., :ch]
            Bm = XBC[..., ch:ch + N]
            Cm = XBC[..., ch + N:]
            cum = jnp.cumsum(jnp.swapaxes(logA, 1, 2), axis=-1)
            diff = cum[..., :, None] - cum[..., None, :]
            causal = jnp.tril(jnp.ones((T, T), dtype=bool))
            A_ss = jnp.where(causal, jnp.exp(jnp.where(causal, diff, 0.0)), 0.0)
            G = jnp.einsum('bihn,bjhn->bhij', Cm, Bm)
            Y = jnp.einsum('bhij,bjhc->bihc', A_ss * G, X)
            gate = jnp.einsum('hoc,bthc->btho', W_gate, x) + b_gate
            Yg = (gate * Y).reshape(B, T, D)
            return Yg @ W_out.T + b_out
        key = jax.random.key(seed)
        ks = jax.random.split(key, 9)
        B, T, D = (2, 256, 256)
        H, ch, N = (H_HEADS, D // H_HEADS, STATE_N)
        inp = jax.random.normal(ks[0], (B, T, D), dtype=jnp.float32)
        W_logA = jax.random.normal(ks[1], (H, 1, ch), dtype=jnp.float32) * 0.01
        b_logA = jnp.full((H, 1), -0.05, dtype=jnp.float32)
        W_XBC = jax.random.normal(ks[3], (H, ch + 2 * N, ch), dtype=jnp.float32) * (1.0 / np.sqrt(ch))
        b_XBC = jax.random.normal(ks[4], (H, ch + 2 * N), dtype=jnp.float32) * 0.02
        W_gate = jax.random.normal(ks[5], (H, ch, ch), dtype=jnp.float32) * (1.0 / np.sqrt(ch))
        b_gate = jax.random.normal(ks[6], (H, ch), dtype=jnp.float32) * 0.02
        W_out = jax.random.normal(ks[7], (D, D), dtype=jnp.float32) * (1.0 / np.sqrt(D))
        b_out = jax.random.normal(ks[8], (D,), dtype=jnp.float32) * 0.02
        return {'inp': inp, 'W_logA': W_logA, 'b_logA': b_logA, 'W_XBC': W_XBC, 'b_XBC': b_XBC, 'W_gate': W_gate, 'b_gate': b_gate, 'W_out': W_out, 'b_out': b_out}
    _L0_attn_all = _L0_attn_setup()
    _L0_attn_in = {k: v for k, v in _L0_attn_all.items() if k in ('W_logA', 'b_logA', 'W_XBC', 'b_XBC', 'W_gate', 'b_gate', 'W_out', 'b_out')}
    del _L0_attn_all

    def _L0_xattn_setup():
        import jax, jax.numpy as jnp
        import numpy as np
        DIM = 256
        HEADS = 16
        HEAD_DIM = DIM // HEADS
        B, N, S = (4, 1024, 128)
        key = jax.random.key(seed)
        ks = jax.random.split(key, 9)
        scale = DIM ** (-0.5)
        return {'x': jax.random.normal(ks[0], (B, N, DIM), dtype=jnp.float32), 'context': jax.random.normal(ks[1], (B, S, DIM), dtype=jnp.float32), 'context_mask': jax.random.uniform(ks[2], (B, S)) < 0.2, 'q_w': jax.random.normal(ks[3], (DIM, DIM), dtype=jnp.float32) * scale, 'q_b': jnp.zeros((DIM,), dtype=jnp.float32), 'kv_w': jax.random.normal(ks[4], (DIM, 2 * DIM), dtype=jnp.float32) * scale, 'kv_b': jnp.zeros((2 * DIM,), dtype=jnp.float32), 'proj_w': jax.random.normal(ks[5], (DIM, DIM), dtype=jnp.float32) * scale, 'proj_b': jnp.zeros((DIM,), dtype=jnp.float32)}
    _L0_xattn_all = _L0_xattn_setup()
    _L0_xattn_in = {k: v for k, v in _L0_xattn_all.items() if k in ('q_w', 'q_b', 'kv_w', 'kv_b', 'proj_w', 'proj_b')}
    del _L0_xattn_all

    def _L0_ffn_setup():
        import jax, jax.numpy as jnp
        import numpy as np
        HIDDEN = 256
        INTER = 1024
        key = jax.random.key(seed)
        k1, k2, k3, k4, k5 = jax.random.split(key, 5)
        hidden_states = jax.random.normal(k1, (4, 512, HIDDEN), dtype=jnp.float32)
        W1 = jax.random.normal(k2, (HIDDEN, INTER), dtype=jnp.float32) * (1.0 / np.sqrt(HIDDEN))
        b1 = jax.random.normal(k3, (INTER,), dtype=jnp.float32) * 0.02
        W2 = jax.random.normal(k4, (INTER, HIDDEN), dtype=jnp.float32) * (1.0 / np.sqrt(INTER))
        b2 = jax.random.normal(k5, (HIDDEN,), dtype=jnp.float32) * 0.02
        return {'hidden_states': hidden_states, 'W1': W1, 'b1': b1, 'W2': W2, 'b2': b2}
    _L0_ffn_all = _L0_ffn_setup()
    _L0_ffn_in = {k: v for k, v in _L0_ffn_all.items() if k in ('W1', 'b1', 'W2', 'b2')}
    del _L0_ffn_all
    return {'x': x, 'ctx_1024': ctx_1024, 'mask_BxS2_bk0': mask_BxS2_bk0, 'L0_attn_W_logA': _L0_attn_in['W_logA'], 'L0_attn_b_logA': _L0_attn_in['b_logA'], 'L0_attn_W_XBC': _L0_attn_in['W_XBC'], 'L0_attn_b_XBC': _L0_attn_in['b_XBC'], 'L0_attn_W_gate': _L0_attn_in['W_gate'], 'L0_attn_b_gate': _L0_attn_in['b_gate'], 'L0_attn_W_out': _L0_attn_in['W_out'], 'L0_attn_b_out': _L0_attn_in['b_out'], 'L0_xattn_q_w': _L0_xattn_in['q_w'], 'L0_xattn_q_b': _L0_xattn_in['q_b'], 'L0_xattn_kv_w': _L0_xattn_in['kv_w'], 'L0_xattn_kv_b': _L0_xattn_in['kv_b'], 'L0_xattn_proj_w': _L0_xattn_in['proj_w'], 'L0_xattn_proj_b': _L0_xattn_in['proj_b'], 'L0_ffn_W1': _L0_ffn_in['W1'], 'L0_ffn_b1': _L0_ffn_in['b1'], 'L0_ffn_W2': _L0_ffn_in['W2'], 'L0_ffn_b2': _L0_ffn_in['b2']}

def reference(x, ctx_1024, mask_BxS2_bk0, L0_attn_W_logA, L0_attn_b_logA, L0_attn_W_XBC, L0_attn_b_XBC, L0_attn_W_gate, L0_attn_b_gate, L0_attn_W_out, L0_attn_b_out, L0_xattn_q_w, L0_xattn_q_b, L0_xattn_kv_w, L0_xattn_kv_b, L0_xattn_proj_w, L0_xattn_proj_b, L0_ffn_W1, L0_ffn_b1, L0_ffn_W2, L0_ffn_b2):
    import jax
    import jax.numpy as jnp

    def _L0_attn_ref(inp, W_logA, b_logA, W_XBC, b_XBC, W_gate, b_gate, W_out, b_out):
        import jax, jax.numpy as jnp
        import numpy as np
        H_HEADS = 16
        STATE_N = 64

        def _mamba2_forward(inp, W_logA, b_logA, W_XBC, b_XBC, W_gate, b_gate, W_out, b_out):
            B, T, D = inp.shape
            H, N = (H_HEADS, STATE_N)
            ch = D // H
            x = inp.reshape(B, T, H, ch)
            logA = jnp.einsum('hoc,bthc->btho', W_logA, x)[..., 0] + b_logA[:, 0]
            XBC = jax.nn.silu(jnp.einsum('hoc,bthc->btho', W_XBC, x) + b_XBC)
            X = XBC[..., :ch]
            Bm = XBC[..., ch:ch + N]
            Cm = XBC[..., ch + N:]
            cum = jnp.cumsum(jnp.swapaxes(logA, 1, 2), axis=-1)
            diff = cum[..., :, None] - cum[..., None, :]
            causal = jnp.tril(jnp.ones((T, T), dtype=bool))
            A_ss = jnp.where(causal, jnp.exp(jnp.where(causal, diff, 0.0)), 0.0)
            G = jnp.einsum('bihn,bjhn->bhij', Cm, Bm)
            Y = jnp.einsum('bhij,bjhc->bihc', A_ss * G, X)
            gate = jnp.einsum('hoc,bthc->btho', W_gate, x) + b_gate
            Yg = (gate * Y).reshape(B, T, D)
            return Yg @ W_out.T + b_out
        return _mamba2_forward(inp, W_logA, b_logA, W_XBC, b_XBC, W_gate, b_gate, W_out, b_out)

    def _L0_xattn_ref(x, context, context_mask, q_w, q_b, kv_w, kv_b, proj_w, proj_b):
        import jax, jax.numpy as jnp
        import numpy as np
        DIM = 256
        HEADS = 16
        HEAD_DIM = DIM // HEADS
        B, N, S = (4, 1024, 128)
        b, n, c = x.shape
        s = context.shape[1]
        h, d = (HEADS, HEAD_DIM)
        scale = d ** (-0.5)
        q = (x @ q_w + q_b).reshape(b, n, h, d)
        kv = (context @ kv_w + kv_b).reshape(b, s, 2, h, d)
        k = kv[:, :, 0]
        v = kv[:, :, 1]
        attn = jnp.einsum('bnhd,bshd->bhns', q, k) * scale
        attn = jnp.where(context_mask[:, None, None, :], -jnp.inf, attn)
        attn = jax.nn.softmax(attn, axis=-1)
        out = jnp.einsum('bhns,bshd->bnhd', attn, v).reshape(b, n, c)
        return out @ proj_w + proj_b

    def _L0_ffn_ref(hidden_states, W1, b1, W2, b2):
        import jax, jax.numpy as jnp
        import numpy as np
        HIDDEN = 256
        INTER = 1024
        h = jax.nn.relu(jnp.einsum('bsh,hi->bsi', hidden_states, W1) + b1)
        return jnp.einsum('bsi,ih->bsh', h, W2) + b2
    x = _layernorm(x + _L0_attn_ref(x, L0_attn_W_logA, L0_attn_b_logA, L0_attn_W_XBC, L0_attn_b_XBC, L0_attn_W_gate, L0_attn_b_gate, L0_attn_W_out, L0_attn_b_out), axis=-1)
    x = _layernorm(x + _L0_xattn_ref(x, ctx_1024, mask_BxS2_bk0, L0_xattn_q_w, L0_xattn_q_b, L0_xattn_kv_w, L0_xattn_kv_b, L0_xattn_proj_w, L0_xattn_proj_b), axis=-1)
    x = _layernorm(x + _L0_ffn_ref(x, L0_ffn_W1, L0_ffn_b1, L0_ffn_W2, L0_ffn_b2), axis=-1)
    return x

_drawn_inputs = setup_inputs


def setup_inputs(seed=0):
    import zlib

    import numpy as np

    out = dict(_drawn_inputs(seed))
    spreads = {'L0_attn_b_logA': (-0.05000000074505806, 0.2),
     'L0_xattn_q_b': (0.0, 0.428),
     'L0_xattn_kv_b': (0.0, 0.1),
     'L0_xattn_proj_b': (0.0, 0.1)}
    factors = {'L0_attn_b_gate': 3.478, 'L0_attn_b_out': 58.526, 'L0_ffn_b1': 4.927, 'L0_ffn_b2': 3.525}
    for name, (base, spread) in spreads.items():
        noise = np.random.default_rng([zlib.crc32(name.encode()), seed]).standard_normal(out[name].shape)
        drawn = base * np.exp(spread * noise) if base else spread * noise
        out[name] = jnp.asarray(drawn.astype(out[name].dtype))
    for name, factor in factors.items():
        out[name] = (out[name] * factor).astype(out[name].dtype)
    return out
```

```python
from contextlib import ExitStack

import numpy as np

import concourse.bass as bass
from concourse import mybir

F = mybir.dt.float32
R = mybir.dt.float32r
U8 = mybir.dt.uint8
ALU = mybir.AluOpType
ACT = mybir.ActivationFunctionType
AX = mybir.AxisListType.X

B, T, D, H, CH, NS, S = 4, 1024, 256, 16, 16, 64, 77
NT = B * T // 128
GT = 2
NG = NT // GT
TPB = T // 128
KX = 98
WT = 66
WCOLS = 2048 + 8 * WT
NEG = -1.0e30
EPS = 1e-5
SCALE = 0.25
HS = H * S
NBLK = 10


FT = 4
NF = NT // FT
GW = 128 * GT


def by_head(ap):
    return ap.rearrange("p (m r c) -> p m r c", r=2, c=16)


def per_head(ap):
    return ap.rearrange("p (r m) -> p m r", r=2).unsqueeze(3).to_broadcast([128, 8, 2, 16])


def heads(q):
    return [8 * (q % 2) + q // 2 + 2 * k for k in range(4)]


def blk_rows(m):
    return min(128, HS - 128 * m)


def blk_heads(m):
    return 128 * m // S, (128 * m + blk_rows(m) - 1) // S


class Token:

    def __init__(self, sem, val):
        self.sem, self.val = sem, val


class Marks:

    def __init__(self, make):
        self.make, self.sems, self.vals = make, {}, {}

    def bump(self, name, by):
        if name not in self.sems:
            self.sems[name] = self.make("s_" + name)
            self.vals[name] = 0
        self.vals[name] += by
        return Token(name, self.vals[name])


class Queue:

    def __init__(self, marks):
        self.marks, self.items, self.seen = marks, [], {}

    def wait(self, *tokens):
        need = {}
        for t in tokens:
            if t is not None:
                need[t.sem] = max(need.get(t.sem, 0), t.val)
        for name, val in need.items():
            if self.seen.get(name, 0) < val:
                self.seen[name] = val
                self.items.append(("wait", name, val))

    def do(self, fn, mark=None, by=1):
        token = self.marks.bump(mark, by) if mark else None
        self.items.append(("do", fn, mark, by))
        return token

    def run(self, eng):
        for it in self.items:
            if it[0] == "wait":
                eng.wait_ge(self.marks.sems[it[1]], it[2])
            else:
                ins = it[1](eng)
                if it[2]:
                    ins.then_inc(self.marks.sems[it[2]], it[3])


class Ring:

    def __init__(self, bufs):
        self.bufs, self.free, self.n = bufs, [()] * len(bufs), 0

    def take(self):
        i = self.n % len(self.bufs)
        self.n += 1
        return i, self.bufs[i], self.free[i]


def build(nc, a, out):
    ctx = ExitStack()
    with ctx:
        def sb(name, shape, dt=F):
            return ctx.enter_context(nc.sbuf_tensor(name, shape, dt))

        marks = Marks(lambda n: ctx.enter_context(nc.semaphore(n)))
        pe, act, dve, pool, sp = (Queue(marks) for _ in range(5))

        banks = [ctx.enter_context(nc.psum_tensor(f"bank{i}", [128, 512], F)) for i in range(8)]
        free_banks = [(b, ()) for b in banks]

        def bank():
            while not free_banks:
                yield
            b, toks = free_banks.pop(0)
            pe.wait(*toks)
            return b

        def release(b, *toks):
            free_banks.append((b, toks))

        wst = sb("wst", [KX, WCOLS], R)
        hT = sb("hT", [128, 8, 512])
        wraw = hT[0:KX, :, :].rearrange("p a b -> p (a b)")[:, 0:WCOLS]
        ident = sb("ident", [128, 128])
        tri = sb("tri", [128, 128])
        ntri = sb("ntri", [128, 128])
        sup = sb("sup", [128, 128])
        ones = sb("ones", [128, 128])
        negm = sb("negm", [128, 1])
        wout = sb("wout", [128, 2, 256])
        qw = sb("qw", [128, 2, 256])
        kvw = hT[:, 6:8, :]
        pw = sb("pw", [128, 2, 256])
        w1 = sb("w1", [128, 2, 1024])
        w2 = sb("w2", [128, 8, 256])
        b1c = sb("b1c", [128, 8])
        qbc = sb("qbc", [128, 2])
        kbc = sb("kbc", [128, 2])
        bo = sb("bo", [128, 256])
        bp = sb("bp", [128, 256])
        b2 = sb("b2", [128, 256])
        mhalf = sb("mhalf", [128, 1])

        P = [sb(f"P{i}", [128, HS]) for i in range(2)]
        PT = [sb(f"PT{i}", [128, NBLK, 128]) for i in range(1)]
        x2s = sb("x2s", [128, 2 * FT, 256])
        x2 = x2s[:, 0:FT, :]
        uT = x2s[:, FT:2 * FT, :].rearrange("p a b -> p (a b)").rearrange("p (a b) -> p a b", a=2)
        ctxT = P[0][:, 0:2 * B * S].rearrange("p (a s) -> p a s", a=2)
        kT = P[0][:, 2 * B * S:4 * B * S].rearrange("p (a s) -> p a s", a=2)
        bv = P[1][0:S, 2 * B * S:2 * B * S + 256]
        khi = P[1][:, 0:2 * B * S].rearrange("p (a s) -> p a s", a=2)
        vt = x2s[0:S, :, :].rearrange("p a b -> p (a b)")[:, 0:B * H * 17].rearrange("p (b h c) -> p b h c", b=B, h=H)
        kst = sb("kst", [97, B, 8, 2 * S], R)
        mrow = sb("mrow", [97, B * S], U8)
        mcol = sb("mcol", [S, B], U8)
        valid = sb("valid", [S, B])
        vb = sb("vb", [128, B, NBLK, 51])

        xT = sb("xT", [128, 2, GW])
        xhi = sb("xhi", [128, 2, GW])
        xst = sb("xst", [KX, 8, GW], R)
        qf = sb("qf", [128, 2, GW])
        qhi = sb("qhi", [128, 2, GW])
        qst = sb("qst", [97, 8, GW], R)
        Bc = sb("Bc", [128, 8, GW])
        Cc = sb("Cc", [128, 8, GW])
        Bt = [sb(f"Bt{i}", [128, 1024]) for i in range(2)]
        Xt = sb("Xt", [128, GT, 256])
        gt = sb("gt", [128, GT, 256])
        la = sb("la", [128, GT, 16])
        DL = [sb(f"DL{i}", [66, 128], R) for i in range(2)]
        RB = [sb(f"RB{i}", [66, 2048], R) for i in range(2)]
        dec = [sb(f"dec{i}", [128, 48]) for i in range(2)]
        E = [sb(f"E{i}", [128, 4, 128]) for i in range(5)]
        Xd = [sb(f"Xd{i}", [128, 256]) for i in range(2)]
        St = [sb(f"St{i}", [128, 8, 32]) for i in range(2)]
        SF = sb("SF", [128, 8, 32])
        xr = [sb(f"xr{i}", [128, 256]) for i in range(2)]
        y1 = [sb(f"y1_{i}", [128, 256]) for i in range(2)]
        yT = [sb(f"yT{i}", [128, 2, 128]) for i in range(2)]
        x1 = sb("x1", [128, GT, 256])
        tT = sb("tT", [128, 2, GW])
        mx = [sb(f"mx{i}", [128, 16]) for i in range(2)]
        rc = [sb(f"rc{i}", [128, 16]) for i in range(2)]
        ob = [sb(f"ob{i}", [128, 256]) for i in range(2)]
        oT = [sb(f"oT{i}", [128, 2, 128]) for i in range(2)]
        res = [sb(f"res{i}", [128, 256]) for i in range(4)]
        st = [sb(f"st{i}", [128, 8]) for i in range(4)]
        rs = [sb(f"rs{i}", [128, 2]) for i in range(4)]

        done = {}

        def need(*keys):
            while any(k not in done for k in keys):
                yield

        r_DL, r_RB, r_dec, r_E, r_Xd, r_St = Ring(DL), Ring(RB), Ring(dec), Ring(E), Ring(Xd), Ring(St)
        r_Bt = Ring(Bt)
        r_xr, r_y1, r_yT, r_mx, r_P, r_PT = Ring(xr), Ring(y1), Ring(yT), Ring(mx), Ring(P), Ring(PT)
        r_rc, r_ob, r_oT, r_res = Ring(rc), Ring(ob), Ring(oT), Ring(res)
        stores = []

        def load(dst, src, mark, **kw):
            return sp.do(lambda e: e.dma_start(dst, src, **kw), mark, 16)

        t_w = load(wraw, a["wst"], "ld_wst")
        t_nm = load(negm[:, :], a["negm"], "ld_negm")
        dlr = PT[0][0:66, 9, :]
        rbr = PT[0][0:66, :, :].rearrange("p a b -> p (a b)")
        rbr2 = x2s[0:66, :, :].rearrange("p a b -> p (a b)")
        t_dl = load(dlr, a["dl"], "ld_dl")
        load(rbr[:, 0:1024], a["rb"][:, 0:1024], "ld_rb")
        t_rb = load(rbr2[:, 0:1024], a["rb"][:, 1024:2048], "ld_rb")
        for dst, name in ((ident, "ident"), (tri, "tri"), (ntri, "ntri"), (sup, "sup"), (ones, "ones"), (mhalf, "mhalf")):
            t_cst = load(dst[:, :], a[name], "ld_cst")

        dve.wait(t_w, t_nm)
        t = dve.do(lambda e: e.tensor_copy(wst[:, :], wraw), "wst_hi")
        dve.wait(t)
        t_wst = dve.do(lambda e: e.scalar_tensor_tensor(
            out=wst[64:KX, :], in0=wst[64:KX, :].bitcast(F), scalar=negm[64:KX, 0:1], in1=wraw[64:KX, :],
            op0=ALU.mult, op1=ALU.add), "wst_lo")
        dve.wait(t_dl, t_rb)
        for i in range(2):
            dve.do(lambda e, i=i: e.tensor_copy(DL[i][:, :], dlr), "dl_init")
            dve.do(lambda e, i=i: e.tensor_copy(RB[i][0:66, 0:1024], rbr[:, 0:1024]), "rb_init")
            t_rbi = dve.do(lambda e, i=i: e.tensor_copy(RB[i][0:66, 1024:2048], rbr2[:, 0:1024]), "rb_init")
        t_dli = Token("dl_init", 2)

        t_x1 = dve.do(lambda e: e.memset(xst[96:98, :, :].bitcast(F), 1.0), "ones_rows")
        t_q1 = dve.do(lambda e: e.memset(qst[96:97, :, :].bitcast(F), 1.0), "ones_rows")
        for i in range(2):
            t_s0 = pool.do(lambda e, i=i: e.memset(St[i][:, :, :], 0.0), "s_zero")
        t_kz = pool.do(lambda e: e.memset(kst[:, :, :, :].bitcast(F), 0.0), "kv_zero")
        t_vz = pool.do(lambda e: e.memset(vb[:, :, :, :], 0.0), "kv_zero")
        pool.wait(t_rbi)
        t_v1 = pool.do(lambda e: e.memset(vt, 1.0), "kv_zero")

        def stack(hi, lo, dst, t_hi, t_lo, waits, mark):
            sp.wait(t_hi, *waits)
            tok = None
            for src, row in ((hi, 0), (hi, 64), (lo, 32)):
                if row == 32:
                    sp.wait(t_lo)
                for q in range(4):
                    d = dst[row:row + 32, q:8:4, :].bitcast(F)
                    s = src[32 * q:32 * q + 32, :, :]
                    tok = sp.do(lambda e, d=d, s=s: e.dma_start(d, s), mark, 16)
            return tok

        xs_tok = {}

        def load_x(g):
            if g:
                sp.wait(xs_tok[g - 1])
            t0 = load(xT[:, :, :], a["xT"][:, :, GW * g:GW * g + GW], "ld_xT")
            yield
            pool.wait(t0, *(([xs_tok[g - 1]]) if g else []))
            t1 = pool.do(lambda e: e.tensor_copy(xhi[:, :, :].bitcast(R), xT[:, :, :]), "x_hi")
            pool.wait(t1)
            t2 = pool.do(lambda e: e.tensor_tensor(xT[:, :, :].bitcast(R), xT[:, :, :], xhi[:, :, :], ALU.subtract), "x_lo")
            yield
            if g:
                yield from need(("P1pe", g - 1))
            w = [done[("P1pe", g - 1)]] if g else [t_x1]
            xs_tok[g] = stack(xhi, xT, xst, t1, t2, w, "x_stack")
            done[("xst", g)] = xs_tok[g]

        def p_load():
            for g in range(NG):
                yield from load_x(g)
                yield

        def p_kv():
            sp_l = [(kvw, "kvw"), (ctxT, "ctxT"), (kbc[:, :], "kb"), (bv[:, :], "bv"),
                    (mcol[:, :], "mcol"), (mrow[96:97, :], "mrow")]
            for dst, name in sp_l:
                t_l = load(dst, a[name], "ld_kv")
            yield
            dve.wait(t_l)
            t_va = dve.do(lambda e: e.tensor_scalar(valid[:, :], mcol[:, :], -1.0, 1.0, ALU.mult, ALU.add), "valid")
            dve.wait(t_kz)
            for b in range(B):
                t_mr = dve.do(lambda e, b=b: e.tensor_scalar(
                    kst[96:97, b, :, :].rearrange("p a (h s) -> p (a h) s", s=S),
                    mrow[96:97, b * S:(b + 1) * S].unsqueeze(1).to_broadcast([1, H, S]), NEG, None, ALU.mult), "mask_row")
            pe.wait(t_l)
            tks = []
            for m in range(2):
                bk = yield from bank()
                for k in range(2):
                    t = pe.do(lambda e, bk=bk, m=m, k=k: e.matmul(bk[:, 0:B * S], kvw[:, k, 128 * m:128 * m + 128],
                              ctxT[:, k, :], start=k == 0, stop=k == 1), "k_mm")
                act.wait(t, t_l)
                t = act.do(lambda e, bk=bk, m=m: e.activation(kT[:, m, :], bk[:, 0:B * S], ACT.Identity,
                           bias=kbc[:, m:m + 1]), "k_bias")
                release(bk, t)
                tks.append(t)
                yield
            pool.wait(*tks)
            t1 = pool.do(lambda e: e.tensor_copy(khi.bitcast(R), kT), "k_hi")
            pool.wait(t1)
            t2 = pool.do(lambda e: e.tensor_tensor(kT.bitcast(R), kT, khi, ALU.subtract), "k_lo")
            sp.wait(t1, t2, t_kz)
            for src, row in ((khi, 0), (khi, 32), (kT, 64)):
                for q in range(4):
                    for h2 in range(2):
                        for m in range(2):
                            d = kst[row + 16 * h2:row + 16 * h2 + 16, :, 4 * m + q, S * h2:S * h2 + S].bitcast(F)
                            s = src[32 * q + 16 * h2:32 * q + 16 * h2 + 16, m, :].rearrange("p (b s) -> p b s", s=S)
                            t_ks = sp.do(lambda e, d=d, s=s: e.dma_start(d, s), "k_stack", 16)
                yield
            dve.wait(t_v1)
            for b in range(B):
                bk = yield from bank()
                for k in range(2):
                    t = pe.do(lambda e, bk=bk, b=b, k=k: e.matmul(bk[0:S, 0:256], ctxT[:, k, b * S:(b + 1) * S],
                              kvw[:, k, 256:512], start=k == 0, stop=k == 1), "v_mm")
                dve.wait(t)
                t = dve.do(lambda e, bk=bk, b=b: e.tensor_tensor(
                    vt[:, b, :, 0:16], bk[0:S, 0:256].rearrange("p (h c) -> p h c", c=16),
                    bv[:, :].rearrange("p (h c) -> p h c", c=16), ALU.add), "v_bias")
                release(bk, t)
                dve.wait(t, t_va)
                t = dve.do(lambda e, b=b: e.tensor_scalar(vt[:, b, :, :], vt[:, b, :, :], valid[:, b:b + 1], None,
                           ALU.mult), "v_ready")
                yield
            sp.wait(t, t_vz)
            for m in range(NBLK):
                lo, hi = blk_heads(m)
                for h in range(lo, hi + 1):
                    r0, r1 = max(S * h, 128 * m), min(S * h + S, 128 * m + blk_rows(m))
                    d = vb[r0 - 128 * m:r1 - 128 * m, :, m, 17 * (h - lo):17 * (h - lo) + 17]
                    s = vt[r0 - S * h:r1 - S * h, :, h, :]
                    t_vs = sp.do(lambda e, d=d, s=s: e.dma_start(d, s), "v_stack", 16)
                yield
            done["kv"] = (t_ks, t_vs, t_mr)

        def p1():
            for g in range(NG):
                yield from need(("xst", g))
                if g:
                    yield from need(("P2", g - 1))
                done[("A", g)] = True
                pe.wait(done[("xst", g)], t_wst)
                for n in range(0, 16, 2):
                    p, dst = n % 8, (Bc if n < 8 else Cc)
                    bk = yield from bank()
                    for j in range(2):
                        t = pe.do(lambda e, bk=bk, n=n + j, p=p + j, j=j: e.matmul(bk[:, GW * j:GW * j + GW],
                                  wst[0:KX, 128 * n:128 * n + 128], xst[0:KX, p, :], start=True, stop=True), "bc_mm")
                    act.wait(t)
                    if n == 0 and g:
                        act.wait(*done[("P2", g - 1)])
                    t = act.do(lambda e, bk=bk, p=p, dst=dst: e.activation(
                        dst[:, p:p + 2, :], bk[:, :].rearrange("p (a b) -> p a b", a=2), ACT.Silu), "bc_silu")
                    release(bk, t)
                    yield
                t_bc = t
                bl = yield from bank()
                for i in range(GT):
                    bx = yield from bank()
                    for p in range(8):
                        w0 = 2048 + WT * p
                        x = xst[0:KX, p, 128 * i:128 * i + 128]
                        pe.do(lambda e, x=x, w0=w0, p=p, bx=bx: e.matmul(bx[:, 64 * p:64 * p + 64], x,
                              wst[0:KX, w0:w0 + 64], start=True, stop=True))
                        t = pe.do(lambda e, x=x, w0=w0, p=p, i=i, bl=bl: e.matmul(
                            bl[:, 16 * i + 2 * p:16 * i + 2 * p + 2], x, wst[0:KX, w0 + 64:w0 + 66],
                            start=True, stop=True), "tok_mm")
                    act.wait(t)
                    t1 = act.do(lambda e, bx=bx, i=i: e.activation(
                        Xt[:, i, :].rearrange("p (a c) -> p a c", c=32),
                        bx[:, :].rearrange("p (a c) -> p a c", c=64)[:, :, 0:32], ACT.Silu), "tok_silu")
                    dve.wait(t1)
                    if g:
                        dve.wait(*done[("P2", g - 1)])
                    t2 = dve.do(lambda e, bx=bx, i=i: e.tensor_copy(
                        gt[:, i, :].rearrange("p (a c) -> p a c", c=32),
                        bx[:, :].rearrange("p (a c) -> p a c", c=64)[:, :, 32:64]), "gate_cp")
                    release(bx, t1, t2)
                    yield
                t_pe = Token("tok_mm", marks.vals["tok_mm"])
                dve.wait(t_pe)
                t2 = dve.do(lambda e, bl=bl: e.tensor_copy(
                    la[:, :, :].rearrange("p a (r m) -> p a r m", r=2),
                    bl[:, 0:16 * GT].rearrange("p (a m r) -> p a r m", r=2, m=8)), "la_cp")
                release(bl, t2)
                done[("P1pe", g)] = t_pe
                done[("P1", g)] = (t_bc, t1, t2)
                yield

        def p2a():
            for n in range(NT):
                g, i = divmod(n, GT)
                yield from need(("P1", g))
                if n >= 2:
                    yield from need(("P2b", n - 2))
                _, dl, f_dl = r_DL.take()
                k_rb, rb, f_rb = r_RB.take()
                _, dc, f_dc = r_dec.take()
                bk = yield from bank()
                pe.wait(*done[("P1", g)], t_cst)
                l = la[:, i, :]
                for c, m in ((0, tri), (16, sup), (32, ones)):
                    pe.do(lambda e, c=c, m=m, l=l, bk=bk: e.matmul(bk[:, c:c + 16], m[:, :], l, start=True, stop=True))
                t = pe.do(lambda e, l=l, bk=bk: e.matmul(bk[0:16, 64:192], l, ntri[:, :], start=True, stop=True), "cum_mm")
                act.wait(t, t_dli, *f_dl, *f_dc)
                t1 = act.do(lambda e, dl=dl, bk=bk: e.copy(dl[0:16, :], bk[0:16, 64:192]), "cum_hi")
                act.do(lambda e, dc=dc, bk=bk: e.activation(dc[:, 0:32], bk[:, 0:32], ACT.Exp), "dec")
                for h2 in range(2):
                    t2 = act.do(lambda e, dc=dc, bk=bk, h2=h2: e.activation(
                        dc[64 * h2:64 * h2 + 64, 32:40], bk[64 * h2:64 * h2 + 64, 32 + 8 * h2:40 + 8 * h2], ACT.Exp), "dec")
                dve.wait(t2, t_dli, *f_dl)
                t3 = dve.do(lambda e, dl=dl, bk=bk: e.tensor_tensor(dl[32:48, :], bk[0:16, 64:192],
                            dl[0:16, :].bitcast(F), ALU.subtract), "cum_lo")
                release(bk, t2, t3)
                sp.wait(t1, t3, t_rbi, *f_rb)
                for row, src in ((64, 0), (65, 32)):
                    t4 = sp.do(lambda e, rb=rb, dl=dl, row=row, src=src: e.dma_start(
                        rb[row:row + 1, :].rearrange("p (h t) -> p h t", h=16).bitcast(F), dl[src:src + 16, :].bitcast(F)), f"cum_rows{k_rb}", 16)
                done[("P2a", n)] = (dl, rb, dc, t1, t2, t3, t4)
                yield

        def p2b():
            state = None
            for n in range(NT):
                g, i = divmod(n, GT)
                first, last = n % TPB == 0, n % TPB == TPB - 1
                yield from need(("P2a", n))
                dl, rb, dc, t_hi, t_dec, t_lo, t_rows = done[("P2a", n)]
                cols = slice(128 * i, 128 * i + 128)
                by = yield from bank()
                pe.wait(*done[("P1", g)], t_cst)
                if not last:
                    _, xd, f_xd = r_Xd.take()
                    pool.wait(t_dec, *done[("P1", g)], *f_xd)
                    t_xd = pool.do(lambda e, xd=xd, i=i, dc=dc: e.tensor_tensor(
                        by_head(xd[:, :]), by_head(Xt[:, i, :]), per_head(dc[:, 16:32]), ALU.mult), "xd")
                if not first:
                    s_old, t_s, k_old = state
                    pe.wait(t_s)
                    for p in range(8):
                        t_in = pe.do(lambda e, p=p, by=by, s_old=s_old, cols=cols: e.matmul(
                            by[:, 256 + 32 * p:288 + 32 * p], Cc[:, p, cols], s_old[:, p, :], start=True, stop=True), "inter_mm")
                    r_St.free[k_old] = (t_in,)
                pend = []
                t_bt = []
                if not last:
                    k_bt, bt, f_bt = r_Bt.take()

                def b_token_major(j):
                    bk = yield from bank()
                    for p in range(4):
                        t = pe.do(lambda e, p=p, cols=cols: e.transpose(bk[:, 128 * p:128 * p + 128], Bc[:, 4 * j + p, cols],
                                  ident[:, :]), "bT_mm")
                    q, m = (act, "bT_a") if j else (dve, "bT_v")
                    q.wait(t, *f_bt)
                    o = bt[:, 512 * j:512 * j + 512]
                    t = q.do(lambda e: (e.copy if j else e.tensor_copy)(o, bk[:, :]), m)
                    release(bk, t)
                    t_bt.append(t)

                def flush(q, eb, k_e, t_e):
                    pe.wait(t_e)
                    for k, h in enumerate(heads(q)):
                        t = pe.do(lambda e, k=k, h=h, eb=eb, by=by, i=i: e.matmul(by[:, 16 * h:16 * h + 16], eb[:, k, :],
                                  Xt[:, i, 16 * h:16 * h + 16], start=True, stop=True), "y_mm")
                    r_E.free[k_e] = (t,)
                    return t

                t_dmm = None
                for q in range(4):
                    k_e, eb, f_e = r_E.take()
                    bd = yield from bank()
                    bg = yield from bank()
                    pe.wait(t_rows, t_hi, t_lo)
                    t_dmm = pe.do(lambda e, q=q, bd=bd, dl=dl, rb=rb: e.matmul(bd[:, :], dl[:, :],
                                  rb[:, 512 * q:512 * q + 512], start=True, stop=True), "diff_mm")
                    act.wait(t_dmm, *f_e)
                    t_ex = act.do(lambda e, eb=eb, bd=bd: e.activation(
                        eb[:, :, :], bd[:, :].rearrange("p (h t) -> p h t", h=4), ACT.Exp), "decay_exp")
                    release(bd, t_ex)
                    for k, h in enumerate(heads(q)):
                        r0 = 64 * (h % 2)
                        t_g = pe.do(lambda e, k=k, h=h, r0=r0, bg=bg, cols=cols: e.matmul(
                            bg[:, 128 * k:128 * k + 128], Bc[r0:r0 + 64, h // 2, cols],
                            Cc[r0:r0 + 64, h // 2, cols], start=True, stop=True), "g_mm")
                    pool.wait(t_ex)
                    t_m = pool.do(lambda e, eb=eb: e.affine_select(
                        out=eb[:, :, :], in_=eb[:, :, :], compare_op=ALU.is_ge, fill=0.0, base=0,
                        pattern=[[0, 4], [1, 128]], channel_multiplier=-1), "causal")
                    dve.wait(t_m, t_g)
                    t_e = dve.do(lambda e, eb=eb, bg=bg: e.tensor_tensor(
                        eb[:, :, :], bg[:, :].rearrange("p (h t) -> p h t", h=4), eb[:, :, :], ALU.mult), "ag")
                    release(bg, t_e)
                    pend.append((q, eb, k_e, t_e))
                    if len(pend) > 2:
                        flush(*pend.pop(0))
                    if q % 2 and not last:
                        yield
                        yield from b_token_major(q // 2)
                    yield
                r_DL.free[(n) % 2] = (t_dmm,)
                r_RB.free[(n) % 2] = (t_dmm,)
                t_last_state = None
                if not last:
                    bs = yield from bank()
                    pe.wait(t_xd, *t_bt)
                    for p in range(8):
                        t_sm = pe.do(lambda e, p=p, bs=bs, bt=bt, xd=xd: e.matmul(
                            bs[:, 32 * p:32 * p + 32], bt[:, 128 * p:128 * p + 128], xd[:, 32 * p:32 * p + 32],
                            start=True, stop=True), "state_mm")
                    r_Xd.free[(r_Xd.n - 1) % 2] = (t_sm,)
                    r_Bt.free[k_bt] = (t_sm,)
                    k_s, s_new, f_s = r_St.take()
                    if first:
                        dve.wait(t_sm, t_s0, *f_s)
                        for h2 in range(2):
                            r = slice(64 * h2, 64 * h2 + 64)
                            c = slice(16 * h2, 16 * h2 + 16)
                            t_s = dve.do(lambda e, r=r, c=c, bs=bs, s_new=s_new: e.tensor_copy(
                                s_new[r, :, c], bs[r, 0:256].rearrange("p (a c) -> p a c", c=32)[:, :, c]), "state")
                    else:
                        pool.wait(t_s, t_dec)
                        if done.get("sf_free"):
                            pool.wait(done["sf_free"])
                        t_sf = pool.do(lambda e, s_old=s_old, dc=dc: e.tensor_tensor(
                            SF[:, :, :], s_old[:, :, :], dc[:, 32:40].unsqueeze(2).to_broadcast([128, 8, 32]),
                            ALU.mult), "state_decay")
                        r_St.free[k_old] = (t_in, t_sf)
                        dve.wait(t_sm, t_sf, t_s0, *f_s)
                        for h2 in range(2):
                            r = slice(64 * h2, 64 * h2 + 64)
                            c = slice(16 * h2, 16 * h2 + 16)
                            t_s = dve.do(lambda e, r=r, c=c, bs=bs, s_new=s_new: e.tensor_tensor(
                                s_new[r, :, c], bs[r, 0:256].rearrange("p (a c) -> p a c", c=32)[:, :, c], SF[r, :, c],
                                ALU.add), "state")
                        done["sf_free"] = t_s
                    release(bs, t_s)
                    state = (s_new, t_s, k_s)
                    yield
                for j in range(len(pend)):
                    t_y = flush(*pend.pop(0))
                    yield
                done[("P2b", n)] = (by, t_y, dc, first, Token("state_decay", marks.vals.get("state_decay", 0)) if not first and not last else None)
                yield

        def layernorm(bk, t_mm, resid, w_res, dst, w_dst, mark):
            k, r, f_r = r_res.take()
            s_, v_ = st[k], rs[k]
            dve.wait(t_mm, *w_res, *f_r)
            t0 = dve.do(lambda e: e.tensor_tensor(r[:, :], bk[:, 0:256], resid, ALU.add), "ln_add")
            release(bk, t0)
            dve.wait(t0)
            t1 = dve.do(lambda e: e.bn_stats(s_[:, 0:6], r[:, :]), "ln_stats")
            dve.wait(t1)
            t2 = dve.do(lambda e: e.bn_aggr(s_[:, 6:8], s_[:, 0:6]), "ln_aggr")
            pool.wait(t2, t_cst)
            t3 = pool.do(lambda e: e.tensor_scalar(v_[:, 0:1], s_[:, 7:8], EPS, None, ALU.add), "ln_eps")
            pool.wait(t3)
            t4 = pool.do(lambda e: e.tensor_tensor(v_[:, 1:2], v_[:, 0:1], mhalf[:, 0:1], ALU.pow), "ln_rstd")
            yield
            dve.wait(t4, *w_dst)
            if dst is None:
                t5 = dve.do(lambda e: e.tensor_scalar(r[:, :], r[:, :], s_[:, 6:7], v_[:, 1:2], ALU.subtract, ALU.mult), mark)
                return t0, t5, k, r
            t5 = dve.do(lambda e: e.tensor_scalar(dst, r[:, :], s_[:, 6:7], v_[:, 1:2], ALU.subtract, ALU.mult), mark)
            r_res.free[k] = (t5,)
            return t0, t5

        def transpose2(src, w_src, dst, w_dst, mark):
            bk = yield from bank()
            pe.wait(t_cst, *w_src)
            for k in range(2):
                t = pe.do(lambda e, k=k: e.transpose(bk[:, 128 * k:128 * k + 128], src[:, 128 * k:128 * k + 128],
                          ident[:, :]), mark + "_pe")
            act.wait(t, *w_dst)
            t2 = act.do(lambda e: e.copy(dst, bk[:, 0:256].rearrange("p (a b) -> p a b", a=2)), mark)
            release(bk, t2)
            return t, t2

        def p2c():
            for dst, name in ((wout, "wout"), (pw, "pw"), (qw, "qw")):
                t_wo = load(dst[:, :, :], a[name], "ld_w")
            for dst, name in ((bo, "bo"), (bp, "bp"), (b2, "b2"), (qbc, "qb")):
                t_wo2 = load(dst[:, :], a[name], "ld_b")
            done["w"] = (t_wo, t_wo2)
            for n in range(NT):
                g, i = divmod(n, GT)
                k_xr, x_, f_x = r_xr.take()
                sp.wait(*f_x)
                t_x = load(x_[:, :], a["x"][128 * n:128 * n + 128, :], f"ld_x{k_xr}")
                pool.wait(t_x, t_wo2)
                t_x = pool.do(lambda e, x_=x_: e.tensor_tensor(x_[:, :], x_[:, :], bo[:, :], ALU.add), "x_bias")
                yield from need(("P2b", n))
                by, t_y, dc, first, t_sd = done[("P2b", n)]
                k_y, y, f_y = r_y1.take()
                dve.wait(t_y, *f_y)
                if first:
                    t = dve.do(lambda e, y=y, by=by, i=i: e.tensor_tensor(y[:, :], by[:, 0:256], gt[:, i, :], ALU.mult), "y_gate")
                    release(by, t)
                    r_dec.free[n % 2] = (t_sd, Token("xd", marks.vals["xd"]))
                else:
                    t = dve.do(lambda e, y=y, by=by, dc=dc: e.tensor_tensor(
                        by_head(y[:, :]), by_head(by[:, 256:512]), per_head(dc[:, 0:16]), ALU.mult), "y_dec")
                    r_dec.free[n % 2] = (t, t_sd, Token("xd", marks.vals["xd"]))
                    dve.wait(t)
                    t = dve.do(lambda e, y=y, by=by: e.tensor_tensor(y[:, :], by[:, 0:256], y[:, :], ALU.add), "y_sum")
                    release(by, t)
                    dve.wait(t)
                    t = dve.do(lambda e, y=y, i=i: e.tensor_tensor(y[:, :], y[:, :], gt[:, i, :], ALU.mult), "y_gate")
                done[("y", n)] = t
                if i == GT - 1:
                    done[("P2", g)] = (t, Token("y_mm", marks.vals["y_mm"]), Token("bT_mm", marks.vals["bT_mm"]),
                                       Token("xd", marks.vals["xd"]), Token("inter_mm", marks.vals.get("inter_mm", 0)))
                yield
                k_t, yt, f_t = r_yT.take()
                t_pe, t_t = yield from transpose2(y, (t,), yt[:, :, :], f_t, "yT")
                r_y1.free[k_y] = (t_pe,)
                yield
                bk = yield from bank()
                pe.wait(t_t, t_wo)
                for k in range(2):
                    t = pe.do(lambda e, k=k, bk=bk, yt=yt: e.matmul(bk[:, 0:256], yt[:, k, :], wout[:, k, :],
                              start=k == 0, stop=k == 1), "wout_mm")
                r_yT.free[k_t] = (t,)
                if i == 0 and g:
                    yield from need(("x1free", g - 1))
                wd = done[("x1free", g - 1)] if g else ()
                t0, t5 = yield from layernorm(bk, t, x_[:, :], (t_x,), x1[:, i, :], wd, "ln1")
                r_xr.free[k_xr] = (t0,)
                done[("x1", n)] = t5
                yield

        def p3q():
            for g in range(NG):
                w_t = done[("q", g - 1)][:1] if g else ()
                for i in range(GT):
                    yield from need(("x1", GT * g + i))
                    t_pe, t_t = yield from transpose2(x1[:, i, :], (done[("x1", GT * g + i)],),
                                                      tT[:, :, 128 * i:128 * i + 128], w_t, "x1T")
                    pool.wait(t_pe, done["w"][1])
                    done[("x1b", GT * g + i)] = pool.do(lambda e, i=i: e.tensor_tensor(
                        x1[:, i, :], x1[:, i, :], bp[:, :], ALU.add), "x1b")
                    yield
                for m in range(2):
                    bk = yield from bank()
                    pe.wait(t_t, *done["w"])
                    for k in range(2):
                        t = pe.do(lambda e, bk=bk, m=m, k=k: e.matmul(bk[:, 0:GW], qw[:, k, 128 * m:128 * m + 128],
                                  tT[:, k, :], start=k == 0, stop=k == 1), "q_mm")
                    act.wait(t, *done["w"])
                    if g:
                        act.wait(done[("q", g - 1)][2])
                    t_q = act.do(lambda e, bk=bk, m=m: e.activation(qf[:, m, :], bk[:, 0:GW], ACT.Identity,
                                 bias=qbc[:, m:m + 1]), "q_bias")
                    release(bk, t_q)
                    yield
                pool.wait(t_q)
                if g:
                    pool.wait(done[("q", g - 1)][2])
                t1 = pool.do(lambda e: e.tensor_copy(qhi[:, :, :].bitcast(R), qf[:, :, :]), "q_hi")
                pool.wait(t1)
                t2 = pool.do(lambda e: e.tensor_tensor(qf[:, :, :].bitcast(R), qf[:, :, :], qhi[:, :, :], ALU.subtract), "q_lo")
                if g:
                    yield from need(("P3pe", g - 1))
                w = [done[("P3pe", g - 1)]] if g else [t_q1]
                t3 = stack(qhi, qf, qst, t1, t2, w, "q_stack")
                done[("q", g)] = (t, t2, t3, t_pe)
                yield

        def p3():
            yield from need("kv", "w")
            t_ks, t_vs, t_mr = done["kv"]
            for n in range(NT):
                g, i = divmod(n, GT)
                b = n // TPB
                yield from need(("q", g))
                k_m, m_, f_m = r_mx.take()
                k_p, pb, f_p = r_P.take()
                pe.wait(done[("q", g)][2], t_ks, t_mr)
                for j in range(3):
                    n0, n1 = 3 * j, min(3 * j + 3, 8)
                    w = (n1 - n0) * 2
                    bk = yield from bank()
                    for p in range(n0, n1):
                        t = pe.do(lambda e, p=p, n0=n0, bk=bk, i=i, b=b: e.matmul(
                            bk[:, 2 * S * (p - n0):2 * S * (p - n0 + 1)], qst[0:97, p, 128 * i:128 * i + 128],
                            kst[0:97, b, p, :], start=True, stop=True), "s_mm")
                    v = bk[:, 0:w * S].rearrange("p (h s) -> p h s", s=S)
                    dve.wait(t, *f_m)
                    t1 = dve.do(lambda e, v=v, m_=m_, n0=n0, w=w: e.tensor_reduce(m_[:, 2 * n0:2 * n0 + w], v, AX, ALU.max), "s_max")
                    dve.wait(t1, *f_p)
                    t2 = dve.do(lambda e, v=v, m_=m_, n0=n0, w=w, pb=pb: e.tensor_tensor(
                        pb[:, 2 * S * n0:2 * S * n0 + w * S].rearrange("p (h s) -> p h s", s=S), v,
                        m_[:, 2 * n0:2 * n0 + w].unsqueeze(2).to_broadcast([128, w, S]), ALU.subtract), "s_sub")
                    release(bk, t2)
                    yield
                r_mx.free[k_m] = (t2,)
                if i == GT - 1:
                    done[("P3pe", g)] = t
                act.wait(t2)
                t3 = act.do(lambda e, pb=pb: e.activation(pb[:, :], pb[:, :], ACT.Exp, scale=SCALE), "p_exp")
                yield
                k_pt, pt, f_pt = r_PT.take()
                pe.wait(t3, t_cst)
                tps = []
                for j in range(3):
                    m0, m1 = 4 * j, min(4 * j + 4, NBLK)
                    bk = yield from bank()
                    for m in range(m0, m1):
                        w = blk_rows(m)
                        t = pe.do(lambda e, m=m, m0=m0, w=w, bk=bk, pb=pb: e.transpose(
                            bk[0:w, 128 * (m - m0):128 * (m - m0) + 128], pb[:, 128 * m:128 * m + w], ident[:, :]), "pT_mm")
                    eng = act if j != 1 else dve
                    eng.wait(t, t_rbi, *f_pt)
                    if j < 2:
                        if eng is act:
                            t4 = act.do(lambda e, m0=m0, m1=m1, bk=bk, pt=pt: e.copy(
                                pt[:, m0:m1, :], bk[:, :].rearrange("p (a b) -> p a b", b=128)), "pT")
                        else:
                            t4 = dve.do(lambda e, m0=m0, m1=m1, bk=bk, pt=pt: e.tensor_copy(
                                pt[:, m0:m1, :], bk[:, :].rearrange("p (a b) -> p a b", b=128)), "pT_v")
                        tps.append(t4)
                        release(bk, t4)
                    else:
                        w = blk_rows(9)
                        act.do(lambda e, bk=bk, pt=pt: e.copy(pt[:, 8, :], bk[:, 0:128]), "pT")
                        t4 = act.do(lambda e, bk=bk, pt=pt, w=w: e.copy(pt[0:w, 9, :], bk[0:w, 128:256]), "pT")
                        tps.append(t4)
                        release(bk, t4)
                    yield
                r_P.free[k_p] = (t,)
                bo_ = yield from bank()
                pe.wait(*tps, t_vs)
                for m in range(NBLK):
                    w = blk_rows(m)
                    lo, hi = blk_heads(m)
                    nh = hi - lo + 1
                    t = pe.do(lambda e, m=m, w=w, lo=lo, nh=nh, bo_=bo_, pt=pt, b=b: e.matmul(
                        bo_[:, 17 * lo:17 * (lo + nh)], pt[0:w, m, :], vb[0:w, b, m, 0:17 * nh],
                        start=m == 0, stop=m == NBLK - 1, skip_group_check=True), "pv_mm")
                r_PT.free[k_pt] = (t,)
                k_r, rc_, f_rc = r_rc.take()
                k_o, o_, f_o = r_ob.take()
                ov = bo_[:, 0:272].rearrange("p (h c) -> p h c", c=17)
                dve.wait(t, *f_rc)
                t1 = dve.do(lambda e, ov=ov, rc_=rc_: e.reciprocal(rc_[:, :], ov[:, :, 16]), "p_rcp")
                dve.wait(t1, *f_o)
                t2 = dve.do(lambda e, ov=ov, rc_=rc_, o_=o_: e.tensor_tensor(
                    o_[:, :].rearrange("p (h c) -> p h c", c=16), ov[:, :, 0:16],
                    rc_[:, :].unsqueeze(2).to_broadcast([128, 16, 16]), ALU.mult), "p_norm")
                r_rc.free[k_r] = (t2,)
                release(bo_, t2)
                yield
                k_t, ot, f_t = r_oT.take()
                t_pe, t_t = yield from transpose2(o_, (t2,), ot[:, :, :], f_t, "oT")
                r_ob.free[k_o] = (t_pe,)
                yield
                bk = yield from bank()
                pe.wait(t_t)
                for k in range(2):
                    t = pe.do(lambda e, k=k, bk=bk, ot=ot: e.matmul(bk[:, 0:256], ot[:, k, :], pw[:, k, :],
                              start=k == 0, stop=k == 1), "proj_mm")
                r_oT.free[k_t] = (t,)
                gf, j = divmod(n, FT)
                if j == 0 and gf:
                    yield from need(("x2free", gf - 1))
                wd = done[("x2free", gf - 1)] if gf else ()
                t0, t5 = yield from layernorm(bk, t, x1[:, i, :], (done[("x1b", n)],), x2[:, j, :], wd, "ln2")
                if i == GT - 1:
                    done[("x1free", g)] = (t0,)
                done[("x2", n)] = t5
                yield

        def p4():
            for dst, name in ((w1, "w1"), (w2, "w2")):
                load(dst[:, :, :], a[name], "ld_ffn")
            t_wf = load(b1c[:, :], a["b1"], "ld_ffn")
            t_f1, t_f2 = None, t_wst
            yield from need("kv")
            act.wait(*done["kv"][1:2])
            for g in range(NF):
                for i in range(4):
                    yield from need(("x2", 4 * g + i))
                    t_pe, t_t = yield from transpose2(x2[:, i, :], (done[("x2", 4 * g + i)],),
                                                      uT[:, :, 128 * i:128 * i + 128], (t_f1,), "x2T")
                    pool.wait(t_pe, done["w"][1])
                    done[("x2b", 4 * g + i)] = pool.do(lambda e, i=i: e.tensor_tensor(
                        x2[:, i, :], x2[:, i, :], b2[:, :], ALU.add), "x2b")
                    yield
                for m in range(8):
                    bk = yield from bank()
                    pe.wait(t_t, t_wf)
                    for k in range(2):
                        t_f1 = pe.do(lambda e, bk=bk, m=m, k=k: e.matmul(bk[:, :], w1[:, k, 128 * m:128 * m + 128],
                                     uT[:, k, :], start=k == 0, stop=k == 1), "ffn1_mm")
                    act.wait(t_f1, t_wf, t_f2)
                    t_r = act.do(lambda e, bk=bk, m=m: e.activation(hT[:, m, :], bk[:, :], ACT.Relu,
                                 bias=b1c[:, m:m + 1]), "relu")
                    release(bk, t_r)
                    yield
                for i in range(4):
                    n = 4 * g + i
                    bk = yield from bank()
                    pe.wait(t_r)
                    for m in range(8):
                        t_f2 = pe.do(lambda e, bk=bk, m=m, i=i: e.matmul(bk[:, 0:256], hT[:, m, 128 * i:128 * i + 128],
                                     w2[:, m, :], start=m == 0, stop=m == 7), "ffn2_mm")
                        if m == 3:
                            yield
                    t0, t5, k_o, o_ = yield from layernorm(bk, t_f2, x2[:, i, :], (done[("x2b", n)],), None, (), "ln3")
                    sp.wait(t5)
                    t = sp.do(lambda e, n=n, o_=o_: e.dma_start(out[128 * n:128 * n + 128, :], o_[:, :]), f"store{k_o}", 16)
                    r_res.free[k_o] = (t,)
                    stores.append(t)
                    yield
                done[("x2free", g)] = (t0,)

        lanes = [p_load(), p_kv(), p1(), p2a(), p2b(), p2c(), p3q(), p3(), p4()]
        stuck = 0
        while lanes:
            before = sum(len(q.items) for q in (pe, act, dve, pool, sp))
            for ln in list(lanes):
                try:
                    next(ln)
                except StopIteration:
                    lanes.remove(ln)
            stuck = 0 if sum(len(q.items) for q in (pe, act, dve, pool, sp)) > before else stuck + 1
            assert stuck < 50, (lanes, [k for k in done if isinstance(k, tuple)][-20:], len(free_banks))
        sp.wait(*stores)

        block = ctx.enter_context(nc.Block())

        @block.sync
        def _(eng):
            sp.run(eng)

        @block.tensor
        def _(eng):
            pe.run(eng)

        @block.vector
        def _(eng):
            dve.run(eng)

        @block.scalar
        def _(eng):
            act.run(eng)

        @block.gpsimd
        def _(eng):
            pool.run(eng)


def stacked_weights(W_XBC, b_XBC, W_gate, b_gate, W_logA, b_logA):
    w = np.zeros((KX, WCOLS), W_XBC.dtype)

    def put(col, h, rows, bias):
        r = 16 * (h % 2)
        for k in range(3):
            w[32 * k + r:32 * k + r + 16, col:col + rows.shape[0]] = rows.T
        w[96:98, col:col + rows.shape[0]] = bias

    for h in range(H):
        p, h2 = divmod(h, 2)
        put(128 * p + 64 * h2, h, W_XBC[h, 16:80], b_XBC[h, 16:80])
        put(1024 + 128 * p + 64 * h2, h, W_XBC[h, 80:144], b_XBC[h, 80:144])
        t = 2048 + WT * p
        put(t + 16 * h2, h, W_XBC[h, 0:16], b_XBC[h, 0:16])
        put(t + 32 + 16 * h2, h, W_gate[h], b_gate[h])
        put(t + 64 + h2, h, W_logA[h], b_logA[h])
    return w


def kernel(x, ctx_1024, mask_BxS2_bk0, L0_attn_W_logA, L0_attn_b_logA, L0_attn_W_XBC, L0_attn_b_XBC,
           L0_attn_W_gate, L0_attn_b_gate, L0_attn_W_out, L0_attn_b_out, L0_xattn_q_w, L0_xattn_q_b,
           L0_xattn_kv_w, L0_xattn_kv_b, L0_xattn_proj_w, L0_xattn_proj_b, L0_ffn_W1, L0_ffn_b1,
           L0_ffn_W2, L0_ffn_b2):
    import concourse.bacc as _bacc
    from concourse.bass_utils import run_bass_kernel_spmd as _run

    f = np.float32
    A = np.asarray

    def kmajor(w):
        w = A(w)
        return w.reshape(-1, 128, w.shape[1]).transpose(1, 0, 2)

    def col(v):
        return A(v).reshape(-1, 128).T

    def rows(v, n):
        return np.broadcast_to(A(v), (n, A(v).shape[0]))

    xf = A(x).reshape(B * T, D)
    kvb = A(L0_xattn_kv_b)
    mask = A(mask_BxS2_bk0)
    idx = np.arange(128)
    tri = (idx[:, None] <= idx[None, :]).astype(f)
    dl = np.zeros((66, 128), f)
    dl[64:66] = -1.0
    rb = np.zeros((66, 16, 128), f)
    for h in range(16):
        rb[h, h] = 1.0
        rb[32 + h, h] = 1.0
    negm = np.zeros((128, 1), f)
    negm[64:97] = -1.0
    arrays = {
        "x": xf,
        "xT": xf.T.reshape(2, 128, B * T).transpose(1, 0, 2),
        "wst": stacked_weights(A(L0_attn_W_XBC), A(L0_attn_b_XBC), A(L0_attn_W_gate), A(L0_attn_b_gate),
                               A(L0_attn_W_logA), A(L0_attn_b_logA)),
        "negm": negm, "dl": dl, "rb": rb.reshape(66, 2048),
        "ident": np.eye(128, dtype=f), "tri": tri, "ntri": -tri,
        "sup": (idx[:, None] > idx[None, :]).astype(f), "ones": np.ones((128, 128), f),
        "mhalf": np.full((128, 1), -0.5, f),
        "wout": kmajor(A(L0_attn_W_out).T), "pw": kmajor(L0_xattn_proj_w), "qw": kmajor(L0_xattn_q_w),
        "kvw": kmajor(L0_xattn_kv_w), "w1": kmajor(L0_ffn_W1), "w2": kmajor(L0_ffn_W2),
        "b1": col(L0_ffn_b1), "qb": col(L0_xattn_q_b), "kb": col(kvb[0:256]),
        "bo": rows(L0_attn_b_out, 128), "bp": rows(L0_xattn_proj_b, 128), "b2": rows(L0_ffn_b2, 128),
        "bv": rows(kvb[256:512], S),
        "ctxT": A(ctx_1024).reshape(B * S, D).T.reshape(2, 128, B * S).transpose(1, 0, 2),
        "mcol": mask.T, "mrow": mask.reshape(1, B * S),
    }
    nc = _bacc.Bacc("TRN2", target_bir_lowering=False, num_devices=1)
    maps, aps = {}, {}
    for name, v in arrays.items():
        v = np.ascontiguousarray(v)
        maps[f"in_{name}"] = v
        aps[name] = nc.dram_tensor(f"in_{name}", v.shape, mybir.dt.from_np(v.dtype), kind="ExternalInput").ap()
    out = nc.dram_tensor("out_0", (B * T, D), F, kind="ExternalOutput").ap()
    build(nc, aps, out)
    r = _run(nc, [maps], core_ids=[0])
    return r.results[0]["out_0"].reshape(B, T, D)
```

```python
from contextlib import ExitStack

import numpy as np

import concourse.bass as bass
from concourse import mybir

F = mybir.dt.float32
R = mybir.dt.float32r
U8 = mybir.dt.uint8
ALU = mybir.AluOpType
ACT = mybir.ActivationFunctionType
AX = mybir.AxisListType.X

B, T, D, H, CH, NS, S = 4, 1024, 256, 16, 16, 64, 77
NT = B * T // 128
GT = 2
NG = NT // GT
TPB = T // 128
KX = 98
WT = 66
WCOLS = 2048 + 8 * WT
NEG = -1.0e30
EPS = 1e-5
SCALE = 0.25
HS = H * S
NBLK = 10


FT = 4
NF = NT // FT
GW = 128 * GT


def by_head(ap):
    return ap.rearrange("p (m r c) -> p m r c", r=2, c=16)


def per_head(ap):
    return ap.rearrange("p (r m) -> p m r", r=2).unsqueeze(3).to_broadcast([128, 8, 2, 16])


def heads(q):
    return [8 * (q % 2) + q // 2 + 2 * k for k in range(4)]


def blk_rows(m):
    return min(128, HS - 128 * m)


def blk_heads(m):
    return 128 * m // S, (128 * m + blk_rows(m) - 1) // S


class Token:

    def __init__(self, sem, val, at=0.0):
        self.sem, self.val, self.at = sem, val, at


class Marks:

    def __init__(self, make):
        self.make, self.sems, self.vals, self.last = make, {}, {}, {}

    def bump(self, name, by, at):
        if name not in self.sems:
            self.sems[name] = self.make("s_" + name)
            self.vals[name] = 0
        self.vals[name] += by
        self.last[name] = Token(name, self.vals[name], at)
        return self.last[name]


class Queue:

    def __init__(self, marks, latency):
        self.marks, self.items, self.seen, self.now, self.latency = marks, [], {}, 0.0, latency

    def start(self, tokens):
        return max([self.now] + [t.at + self.latency for t in tokens if t is not None])

    def wait(self, *tokens):
        self.now = self.start(tokens)
        need = {}
        for t in tokens:
            if t is not None:
                need[t.sem] = max(need.get(t.sem, 0), t.val)
        for name, val in need.items():
            if self.seen.get(name, 0) < val:
                self.seen[name] = val
                self.items.append(("wait", name, val))

    def do(self, fn, mark=None, by=1, ns=0.0):
        if by == 16:
            self.now += 60.0
            token = self.marks.bump(mark, by, self.now + 2500.0)
        else:
            self.now += ns
            token = self.marks.bump(mark, by, self.now) if mark else None
        self.items.append(("do", fn, mark, by))
        return token

    def run(self, eng):
        for it in self.items:
            if it[0] == "wait":
                eng.wait_ge(self.marks.sems[it[1]], it[2])
            else:
                ins = it[1](eng)
                if it[2]:
                    ins.then_inc(self.marks.sems[it[2]], it[3])


def at(queue, *tokens):
    yield queue, tokens
    queue.wait(*tokens)


BLOCKED = (None, ())


def interleave(lanes, queues):
    state = {ln: next(ln) for ln in lanes}
    idle = 0
    while lanes:
        for ln in list(lanes):
            if state[ln][0] is None:
                try:
                    state[ln] = next(ln)
                except StopIteration:
                    lanes.remove(ln)
        best, when = None, None
        for ln in lanes:
            q, toks = state[ln]
            if q is not None:
                t = q.start(toks)
                if best is None or t < when - 1.0:
                    best, when = ln, t
        if best is None:
            idle += 1
            assert idle < 100, "no lane can go on"
            continue
        idle = 0
        try:
            state[best] = next(best)
        except StopIteration:
            lanes.remove(best)


class Ring:

    def __init__(self, bufs, first=()):
        self.bufs, self.free, self.n = bufs, [first] * len(bufs), 0

    def take(self):
        i = self.n % len(self.bufs)
        while self.free[i] is None:
            yield BLOCKED
            i = self.n % len(self.bufs)
        self.n += 1
        was, self.free[i] = self.free[i], None
        return i, self.bufs[i], was


def mm(n):
    return 4 * max(64, n) / 2.4


def mmr(n):
    return max(60, n) / 2.4


def ac(n):
    return 190 + n / 1.2


def ve(n, fast=False):
    return 70 + n / (1.92 if fast else 0.96)


def build(nc, a, out):
    ctx = ExitStack()
    with ctx:
        def sb(name, shape, dt=F):
            return ctx.enter_context(nc.sbuf_tensor(name, shape, dt))

        marks = Marks(lambda n: ctx.enter_context(nc.semaphore(n)))
        pe, act, dve, pool, sp = (Queue(marks, 120.0) for _ in range(5))
        last = marks.last

        banks = [ctx.enter_context(nc.psum_tensor(f"bank{i}", [128, 512], F)) for i in range(8)]
        free_banks = [(b, ()) for b in banks]

        def bank():
            while not free_banks:
                yield BLOCKED
            free_banks.sort(key=lambda f: pe.start(f[1]))
            b, toks = free_banks.pop(0)
            pe.wait(*toks)
            return b

        def release(b, *toks):
            free_banks.append((b, toks))

        wst = sb("wst", [KX, WCOLS], R)
        hT = sb("hT", [128, 8, 512])
        wraw = hT[0:KX, :, :].rearrange("p a b -> p (a b)")[:, 0:WCOLS]
        ident = sb("ident", [128, 128])
        tri = sb("tri", [128, 128])
        sup = sb("sup", [128, 128])
        ones = sb("ones", [128, 128])
        negm = sb("negm", [128, 1])
        wout = sb("wout", [128, 2, 256])
        qw = sb("qw", [128, 2, 256])
        kvw = hT[:, 6:8, :]
        pw = sb("pw", [128, 2, 256])
        w1 = sb("w1", [128, 2, 1024])
        w2 = sb("w2", [128, 8, 256])
        b1c = sb("b1c", [128, 8])
        qbc = sb("qbc", [128, 2])
        kbc = sb("kbc", [128, 2])
        bo = sb("bo", [128, 256])
        bp = sb("bp", [128, 256])
        b2 = sb("b2", [128, 256])
        mhalf = sb("mhalf", [128, 1])

        P = [sb(f"P{i}", [128, HS]) for i in range(2)]
        PT = [sb(f"PT{i}", [128, NBLK, 128]) for i in range(1)]
        x2s = sb("x2s", [128, 2 * FT, 256])
        x2 = x2s[:, 0:FT, :]
        uT = x2s[:, FT:2 * FT, :].rearrange("p a b -> p (a b)").rearrange("p (a b) -> p a b", a=2)
        ctxT = P[0][:, 0:2 * B * S].rearrange("p (a s) -> p a s", a=2)
        kT = P[0][:, 2 * B * S:4 * B * S].rearrange("p (a s) -> p a s", a=2)
        bv = P[1][0:S, 2 * B * S:2 * B * S + 256]
        khi = P[1][:, 0:2 * B * S].rearrange("p (a s) -> p a s", a=2)
        vt = x2s[0:S, :, :].rearrange("p a b -> p (a b)")[:, 0:B * H * 17].rearrange("p (b h c) -> p b h c", b=B, h=H)
        kst = sb("kst", [97, B, 8, 2 * S], R)
        mrow = sb("mrow", [97, B * S], U8)
        mcol = sb("mcol", [S, B], U8)
        valid = sb("valid", [S, B])
        vb = sb("vb", [128, B, NBLK, 51])

        xT = sb("xT", [128, 2, GW])
        xhi = sb("xhi", [128, 2, GW])
        xst = sb("xst", [KX, 8, GW], R)
        qf = sb("qf", [128, 2, GW])
        qhi = sb("qhi", [128, 2, GW])
        qst = sb("qst", [97, 8, GW], R)
        Bc = sb("Bc", [128, 8, GW])
        Cc = sb("Cc", [128, 8, GW])
        Bt = [sb(f"Bt{i}", [128, 1024]) for i in range(2)]
        Xt = sb("Xt", [128, GT, 256])
        gt = sb("gt", [128, GT, 256])
        la = sb("la", [128, GT, 16])
        DL = [sb(f"DL{i}", [66, 128], R) for i in range(2)]
        RB = [sb(f"RB{i}", [66, 2048], R) for i in range(2)]
        dec = [sb(f"dec{i}", [128, 48]) for i in range(2)]
        E = [sb(f"E{i}", [128, 4, 128]) for i in range(5)]
        Xd = [sb(f"Xd{i}", [128, 256]) for i in range(2)]
        St = [sb(f"St{i}", [128, 8, 32]) for i in range(2)]
        SF = sb("SF", [128, 8, 32])
        xr = [sb(f"xr{i}", [128, 256]) for i in range(2)]
        y1 = [sb(f"y1_{i}", [128, 256]) for i in range(2)]
        yT = [sb(f"yT{i}", [128, 2, 128]) for i in range(2)]
        x1 = sb("x1", [128, 4, 256])
        tT = sb("tT", [128, 2, GW])
        mx = [sb(f"mx{i}", [128, 16]) for i in range(2)]
        rc = [sb(f"rc{i}", [128, 16]) for i in range(2)]
        ob = [sb(f"ob{i}", [128, 256]) for i in range(2)]
        oT = [sb(f"oT{i}", [128, 2, 128]) for i in range(2)]
        res = [sb(f"res{i}", [128, 256]) for i in range(3)]
        st = [sb(f"st{i}", [128, 10]) for i in range(6)]

        done = {}

        def need(*keys):
            while any(k not in done for k in keys):
                yield BLOCKED

        r_DL, r_RB, r_dec, r_E, r_Xd, r_St = Ring(DL), Ring(RB), Ring(dec), Ring(E), Ring(Xd), Ring(St)
        r_xr, r_y1, r_yT, r_mx, r_P, r_PT = Ring(xr), Ring(y1), Ring(yT), Ring(mx), Ring(P), Ring(PT)
        r_rc, r_ob, r_oT, r_res, r_st, r_Bt = Ring(rc), Ring(ob), Ring(oT), Ring(res), Ring(st), Ring(Bt)
        silu = [False]

        def exp_turn():
            while silu[0]:
                yield BLOCKED

        def load(dst, src, mark, **kw):
            return sp.do(lambda e: e.dma_start(dst, src, **kw), mark, 16)

        t_w = load(wraw, a["wst"], "ld_wst")
        t_nm = load(negm[:, :], a["negm"], "ld_negm")
        dlr = PT[0][0:66, 9, :]
        rbr = PT[0][0:66, :, :].rearrange("p a b -> p (a b)")
        rbr2 = x2s[0:66, :, :].rearrange("p a b -> p (a b)")
        t_dl = load(dlr, a["dl"], "ld_dl")
        load(rbr[:, 0:1024], a["rb"][:, 0:1024], "ld_rb")
        t_rb = load(rbr2[:, 0:1024], a["rb"][:, 1024:2048], "ld_rb")
        for dst, name in ((ident, "ident"), (tri, "tri"), (sup, "sup"), (ones, "ones"), (mhalf, "mhalf")):
            t_cst = load(dst[:, :], a[name], "ld_cst")

        dve.wait(t_w, t_nm)
        t = dve.do(lambda e: e.tensor_copy(wst[:, :], wraw), "wst_hi")
        dve.wait(t)
        t_wst = dve.do(lambda e: e.scalar_tensor_tensor(
            out=wst[64:KX, :], in0=wst[64:KX, :].bitcast(F), scalar=negm[64:KX, 0:1], in1=wraw[64:KX, :],
            op0=ALU.mult, op1=ALU.add), "wst_lo")
        dve.wait(t_dl, t_rb)
        for i in range(2):
            dve.do(lambda e, i=i: e.tensor_copy(DL[i][:, :], dlr), "dl_init")
            dve.do(lambda e, i=i: e.tensor_copy(RB[i][0:66, 0:1024], rbr[:, 0:1024]), "rb_init")
            t_rbi = dve.do(lambda e, i=i: e.tensor_copy(RB[i][0:66, 1024:2048], rbr2[:, 0:1024]), "rb_init")
        t_dli = Token("dl_init", 2)

        t_x1 = dve.do(lambda e: e.memset(xst[96:98, :, :].bitcast(F), 1.0), "ones_rows")
        t_q1 = dve.do(lambda e: e.memset(qst[96:97, :, :].bitcast(F), 1.0), "ones_rows")
        for i in range(2):
            t_s0 = pool.do(lambda e, i=i: e.memset(St[i][:, :, :], 0.0), "s_zero")
        t_kz = pool.do(lambda e: e.memset(kst[:, :, :, :].bitcast(F), 0.0), "kv_zero")
        t_vz = pool.do(lambda e: e.memset(vb[:, :, :, :], 0.0), "kv_zero")
        pool.wait(t_rbi)
        t_v1 = pool.do(lambda e: e.memset(vt, 1.0), "kv_zero")

        def stack(hi, lo, dst, t_hi, t_lo, waits, mark):
            sp.wait(t_hi, *waits)
            tok = None
            for src, row in ((hi, 0), (hi, 64), (lo, 32)):
                if row == 32:
                    sp.wait(t_lo)
                for q in range(4):
                    d = dst[row:row + 32, q:8:4, :].bitcast(F)
                    s = src[32 * q:32 * q + 32, :, :]
                    tok = sp.do(lambda e, d=d, s=s: e.dma_start(d, s), mark, 16)
            return tok

        def p_load():
            t3 = None
            for g in range(NG):
                yield from at(sp, t3)
                t0 = load(xT[:, :, :], a["xT"][:, :, GW * g:GW * g + GW], "ld_xT")
                yield from at(pool, t0, t3)
                t1 = pool.do(lambda e: e.tensor_copy(xhi[:, :, :].bitcast(R), xT[:, :, :]), "x_hi", ns=1830)
                yield from at(pool, t1)
                t2 = pool.do(lambda e: e.tensor_tensor(xT[:, :, :].bitcast(R), xT[:, :, :], xhi[:, :, :], ALU.subtract),
                             "x_lo", ns=1230)
                if g:
                    yield from need(("P1pe", g - 1))
                w = [done[("P1pe", g - 1)]] if g else [t_x1]
                yield from at(sp, t2, *w)
                t3 = done[("xst", g)] = stack(xhi, xT, xst, t1, t2, w, "x_stack")

        def p_kv():
            sp_l = [(kvw, "kvw"), (ctxT, "ctxT"), (kbc[:, :], "kb"), (bv[:, :], "bv"),
                    (mcol[:, :], "mcol"), (mrow[96:97, :], "mrow")]
            for dst, name in sp_l:
                t_l = load(dst, a[name], "ld_kv")
            yield BLOCKED
            dve.wait(t_l)
            t_va = dve.do(lambda e: e.tensor_scalar(valid[:, :], mcol[:, :], -1.0, 1.0, ALU.mult, ALU.add), "valid")
            dve.wait(t_kz)
            for b in range(B):
                t_mr = dve.do(lambda e, b=b: e.tensor_scalar(
                    kst[96:97, b, :, :].rearrange("p a (h s) -> p (a h) s", s=S),
                    mrow[96:97, b * S:(b + 1) * S].unsqueeze(1).to_broadcast([1, H, S]), NEG, None, ALU.mult), "mask_row")
            pe.wait(t_l)
            tks = []
            for m in range(2):
                bk = yield from bank()
                for k in range(2):
                    t = pe.do(lambda e, bk=bk, m=m, k=k: e.matmul(bk[:, 0:B * S], kvw[:, k, 128 * m:128 * m + 128],
                              ctxT[:, k, :], start=k == 0, stop=k == 1), "k_mm", ns=mm(308))
                act.wait(t, t_l)
                t = act.do(lambda e, bk=bk, m=m: e.activation(kT[:, m, :], bk[:, 0:B * S], ACT.Identity,
                           bias=kbc[:, m:m + 1]), "k_bias", ns=450)
                release(bk, t)
                tks.append(t)
                yield BLOCKED
            pool.wait(*tks)
            t1 = pool.do(lambda e: e.tensor_copy(khi.bitcast(R), kT), "k_hi", ns=2200)
            pool.wait(t1)
            t2 = pool.do(lambda e: e.tensor_tensor(kT.bitcast(R), kT, khi, ALU.subtract), "k_lo", ns=1450)
            sp.wait(t1, t2, t_kz)
            for src, row in ((khi, 0), (khi, 32), (kT, 64)):
                for q in range(4):
                    for h2 in range(2):
                        for m in range(2):
                            d = kst[row + 16 * h2:row + 16 * h2 + 16, :, 4 * m + q, S * h2:S * h2 + S].bitcast(F)
                            s = src[32 * q + 16 * h2:32 * q + 16 * h2 + 16, m, :].rearrange("p (b s) -> p b s", s=S)
                            t_ks = sp.do(lambda e, d=d, s=s: e.dma_start(d, s), "k_stack", 16)
                yield BLOCKED
            dve.wait(t_v1)
            for b in range(B):
                bk = yield from bank()
                for k in range(2):
                    t = pe.do(lambda e, bk=bk, b=b, k=k: e.matmul(bk[0:S, 0:256], ctxT[:, k, b * S:(b + 1) * S],
                              kvw[:, k, 256:512], start=k == 0, stop=k == 1), "v_mm", ns=mm(256))
                dve.wait(t)
                t = dve.do(lambda e, bk=bk, b=b: e.tensor_tensor(
                    vt[:, b, :, 0:16], bk[0:S, 0:256].rearrange("p (h c) -> p h c", c=16),
                    bv[:, :].rearrange("p (h c) -> p h c", c=16), ALU.add), "v_bias", ns=340)
                release(bk, t)
                dve.wait(t, t_va)
                t = dve.do(lambda e, b=b: e.tensor_scalar(vt[:, b, :, :], vt[:, b, :, :], valid[:, b:b + 1], None,
                           ALU.mult), "v_ready")
                yield BLOCKED
            sp.wait(t, t_vz)
            for m in range(NBLK):
                lo, hi = blk_heads(m)
                for h in range(lo, hi + 1):
                    r0, r1 = max(S * h, 128 * m), min(S * h + S, 128 * m + blk_rows(m))
                    d = vb[r0 - 128 * m:r1 - 128 * m, :, m, 17 * (h - lo):17 * (h - lo) + 17]
                    s = vt[r0 - S * h:r1 - S * h, :, h, :]
                    t_vs = sp.do(lambda e, d=d, s=s: e.dma_start(d, s), "v_stack", 16)
                yield BLOCKED
            done["kv"] = (t_ks, t_vs, t_mr)

        def p1():
            for g in range(NG):
                yield from need(("xst", g))
                if g:
                    yield from need(*((("P2", n) for n in range(GT * (g - 1), GT * g))))
                w_free = tuple(t for n in range(GT * (g - 1), GT * g) for t in done[("P2", n)]) if g else ()
                for n in range(0, 16, 2):
                    p, dst = n % 8, (Bc if n < 8 else Cc)
                    yield from at(pe, done[("xst", g)], t_wst)
                    bk = yield from bank()
                    for j in range(2):
                        t = pe.do(lambda e, bk=bk, n=n + j, p=p + j, j=j: e.matmul(bk[:, GW * j:GW * j + GW],
                                  wst[0:KX, 128 * n:128 * n + 128], xst[0:KX, p, :], start=True, stop=True),
                                  "bc_mm", ns=mmr(GW))
                    silu[0] = True
                    yield from at(act, t, *w_free)
                    t_bc = act.do(lambda e, bk=bk, p=p, dst=dst: e.activation(
                        dst[:, p:p + 2, :], bk[:, :].rearrange("p (a b) -> p a b", a=2), ACT.Silu), "bc_silu", ns=ac(512))
                    release(bk, t_bc)
                yield from at(pe)
                bl = yield from bank()
                for i in range(GT):
                    yield from at(pe)
                    bx = yield from bank()
                    for p in range(8):
                        w0 = 2048 + WT * p
                        x = xst[0:KX, p, 128 * i:128 * i + 128]
                        pe.do(lambda e, x=x, w0=w0, p=p, bx=bx: e.matmul(bx[:, 64 * p:64 * p + 64], x,
                              wst[0:KX, w0:w0 + 64], start=True, stop=True), ns=30)
                        t = pe.do(lambda e, x=x, w0=w0, p=p, i=i, bl=bl: e.matmul(
                            bl[:, 16 * i + 2 * p:16 * i + 2 * p + 2], x, wst[0:KX, w0 + 64:w0 + 66],
                            start=True, stop=True), "tok_mm", ns=25)
                    if i == GT - 1:
                        t_pe = t
                    yield from at(act, t)
                    t1 = act.do(lambda e, bx=bx, i=i: e.activation(
                        Xt[:, i, :].rearrange("p (a c) -> p a c", c=32),
                        bx[:, :].rearrange("p (a c) -> p a c", c=64)[:, :, 0:32], ACT.Silu), "tok_silu", ns=ac(256))
                    if i == GT - 1:
                        silu[0] = False
                    yield from at(dve, t1, *w_free)
                    t2 = dve.do(lambda e, bx=bx, i=i: e.tensor_copy(
                        gt[:, i, :].rearrange("p (a c) -> p a c", c=32),
                        bx[:, :].rearrange("p (a c) -> p a c", c=64)[:, :, 32:64]), "gate_cp", ns=ve(256))
                    release(bx, t1, t2)
                yield from at(dve, t_pe)
                t2 = dve.do(lambda e, bl=bl: e.tensor_copy(
                    la[:, :, :].rearrange("p a (r m) -> p a r m", r=2),
                    bl[:, 0:16 * GT].rearrange("p (a m r) -> p a r m", r=2, m=8)), "la_cp", ns=120)
                release(bl, t2)
                done[("P1pe", g)] = t_pe
                done[("P1", g)] = (t_bc, t1, t2)

        def p2a():
            for n in range(NT):
                g, i = divmod(n, GT)
                yield from need(("P1", g))
                k_dl, dl, f_dl = yield from r_DL.take()
                k_rb, rb, f_rb = yield from r_RB.take()
                k_dc, dc, f_dc = yield from r_dec.take()
                yield from at(pe, *done[("P1", g)], t_cst)
                bk = yield from bank()
                l = la[:, i, :]
                for c, m in ((0, tri), (16, sup), (32, ones)):
                    pe.do(lambda e, c=c, m=m, l=l, bk=bk: e.matmul(bk[:, c:c + 16], m[:, :], l, start=True, stop=True),
                          ns=mm(16))
                t = pe.do(lambda e, l=l, bk=bk: e.matmul(bk[0:16, 64:192], l, tri[:, :], start=True, stop=True),
                          "cum_mm", ns=mm(128))
                yield from exp_turn()
                yield from at(act, t, t_dli, *f_dl, *f_dc)
                t1 = act.do(lambda e, dl=dl, bk=bk: e.copy(dl[0:16, :], bk[0:16, 64:192]), "cum_hi", ns=ac(128))
                act.do(lambda e, dc=dc, bk=bk: e.activation(dc[:, 0:32], bk[:, 0:32], ACT.Exp), "dec", ns=220)
                for h2 in range(2):
                    t2 = act.do(lambda e, dc=dc, bk=bk, h2=h2: e.activation(
                        dc[64 * h2:64 * h2 + 64, 32:40], bk[64 * h2:64 * h2 + 64, 32 + 8 * h2:40 + 8 * h2], ACT.Exp),
                        "dec", ns=200)
                yield from at(dve, t2, t_dli, *f_dl)
                t3 = dve.do(lambda e, dl=dl, bk=bk: e.tensor_tensor(dl[32:48, :], bk[0:16, 64:192],
                            dl[0:16, :].bitcast(F), ALU.subtract), "cum_lo", ns=ve(128))
                release(bk, t2, t3)
                yield from at(sp, t1, t3, t_rbi, *f_rb)
                for row, src in ((64, 0), (65, 32)):
                    t4 = sp.do(lambda e, rb=rb, dl=dl, row=row, src=src: e.dma_start(
                        rb[row:row + 1, :].rearrange("p (h t) -> p h t", h=16).bitcast(F), dl[src:src + 16, :].bitcast(F)),
                        f"cum_rows{k_rb}", 16)
                done[("P2a", n)] = (dl, rb, dc, t1, t2, t3, t4, k_dl, k_rb, k_dc)

        def p2g(lane, lanes_):
            for s in range(lane, 4 * NT, lanes_):
                n, q = divmod(s, 4)
                g, i = divmod(n, GT)
                yield from need(("P2a", n))
                if s >= lanes_:
                    yield from need(("g_start", s - 1))
                dl, rb, dc, t_hi, t_dec, t_lo, t_rows, k_dl, k_rb, _ = done[("P2a", n)]
                cols = slice(128 * i, 128 * i + 128)
                k_e, eb, f_e = yield from r_E.take()
                done[("g_start", s)] = True
                yield from at(pe, t_rows, t_hi, t_lo)
                bd = yield from bank()
                t_d = pe.do(lambda e, q=q, bd=bd, dl=dl, rb=rb: e.matmul(bd[:, :], dl[:, :],
                            rb[:, 512 * q:512 * q + 512], start=True, stop=True), "diff_mm", ns=mmr(512))
                if q == 3:
                    r_DL.free[k_dl] = r_RB.free[k_rb] = (t_d,)
                yield from at(pe, *done[("P1", g)])
                bg = yield from bank()
                for k, h in enumerate(heads(q)):
                    r0 = 64 * (h % 2)
                    t_g = pe.do(lambda e, k=k, h=h, r0=r0, bg=bg, cols=cols: e.matmul(
                        bg[:, 128 * k:128 * k + 128], Bc[r0:r0 + 64, h // 2, cols],
                        Cc[r0:r0 + 64, h // 2, cols], start=True, stop=True), "g_mm", ns=mm(128))
                yield from exp_turn()
                yield from at(act, t_d, *f_e)
                t_ex = act.do(lambda e, eb=eb, bd=bd: e.activation(
                    eb[:, :, :], bd[:, :].rearrange("p (h t) -> p h t", h=4), ACT.Exp), "decay_exp", ns=ac(512))
                release(bd, t_ex)
                yield from at(pool, t_ex)
                t_m = pool.do(lambda e, eb=eb: e.affine_select(
                    out=eb[:, :, :], in_=eb[:, :, :], compare_op=ALU.is_ge, fill=0.0, base=0,
                    pattern=[[0, 4], [1, 128]], channel_multiplier=-1), "causal", ns=600)
                yield from at(dve, t_m, t_g)
                t_e = dve.do(lambda e, eb=eb, bg=bg: e.tensor_tensor(
                    eb[:, :, :], bg[:, :].rearrange("p (h t) -> p h t", h=4), eb[:, :, :], ALU.mult), "ag", ns=ve(512))
                release(bg, t_e)
                done[("E", n, q)] = (k_e, eb, t_e)

        def p2y():
            for n in range(NT):
                g, i = divmod(n, GT)
                cols = slice(128 * i, 128 * i + 128)
                yield from need(("E", n, 0))
                yield from at(pe, done[("E", n, 0)][2])
                by = yield from bank()
                t_in = None
                for q in range(4):
                    yield from need(("E", n, q))
                    k_e, eb, t_e = done[("E", n, q)]
                    yield from at(pe, t_e)
                    for k, h in enumerate(heads(q)):
                        t = pe.do(lambda e, k=k, h=h, eb=eb, by=by, i=i: e.matmul(by[:, 16 * h:16 * h + 16], eb[:, k, :],
                                  Xt[:, i, 16 * h:16 * h + 16], start=True, stop=True), "y_mm", ns=mm(16))
                    r_E.free[k_e] = (t,)
                if n % TPB:
                    yield from need(("state", n - 1))
                    s_old, t_s, k_s, keep = done[("state", n - 1)]
                    yield from at(pe, t_s)
                    for p in range(8):
                        t_in = pe.do(lambda e, p=p, by=by, s_old=s_old, cols=cols: e.matmul(
                            by[:, 256 + 32 * p:288 + 32 * p], Cc[:, p, cols], s_old[:, p, :], start=True, stop=True),
                            "inter_mm", ns=mm(32))
                    done[("s_read", n - 1)] = t_in
                done[("P2y", n)] = (by, (t, t_in))

        def p2s():
            t_sf_read = None
            for n in range(NT):
                g, i = divmod(n, GT)
                if n % TPB == TPB - 1:
                    done[("P2s", n)] = (None, None)
                    yield from need(("s_read", n - 1))
                    r_St.free[done[("state", n - 1)][2]] = (done[("s_read", n - 1)],)
                    continue
                yield from need(("P2a", n))
                dc, t_dec = done[("P2a", n)][2], done[("P2a", n)][4]
                cols = slice(128 * i, 128 * i + 128)
                k_xd, xd, f_xd = yield from r_Xd.take()
                yield from at(pool, t_dec, *done[("P1", g)], *f_xd)
                t_xd = pool.do(lambda e, xd=xd, i=i, dc=dc: e.tensor_tensor(
                    by_head(xd[:, :]), by_head(Xt[:, i, :]), per_head(dc[:, 16:32]), ALU.mult), "xd", ns=580)
                k_bt, bt, f_bt = yield from r_Bt.take()
                t_bt = []
                for j in range(2):
                    yield from at(pe, *done[("P1", g)], t_cst)
                    bk = yield from bank()
                    for p in range(4):
                        t_b = pe.do(lambda e, p=p, j=j, bk=bk, cols=cols: e.transpose(
                            bk[:, 128 * p:128 * p + 128], Bc[:, 4 * j + p, cols], ident[:, :]), "bT_mm", ns=60)
                    q, m = (act, "bT_a") if j else (dve, "bT_v")
                    yield from at(q, t_b, *f_bt)
                    o = bt[:, 512 * j:512 * j + 512]
                    t = q.do(lambda e, j=j, o=o, bk=bk: (e.copy if j else e.tensor_copy)(o, bk[:, :]), m, ns=600)
                    release(bk, t)
                    t_bt.append(t)
                yield from at(pe, t_xd, *t_bt)
                bs = yield from bank()
                for p in range(8):
                    t_sm = pe.do(lambda e, p=p, bs=bs, bt=bt, xd=xd: e.matmul(
                        bs[:, 32 * p:32 * p + 32], bt[:, 128 * p:128 * p + 128], xd[:, 32 * p:32 * p + 32],
                        start=True, stop=True), "state_mm", ns=mm(32))
                r_Xd.free[k_xd] = (t_sm,)
                r_Bt.free[k_bt] = (t_sm,)
                k_s, s_new, f_s = yield from r_St.take()
                t_sf = None
                if n % TPB:
                    s_old, t_s, k_old, _ = done[("state", n - 1)]
                    yield from at(pool, t_s, t_dec, t_sf_read)
                    t_sf = pool.do(lambda e, s_old=s_old, dc=dc: e.tensor_tensor(
                        SF[:, :, :], s_old[:, :, :], dc[:, 32:40].unsqueeze(2).to_broadcast([128, 8, 32]),
                        ALU.mult), "state_decay", ns=580)
                yield from at(dve, t_sm, t_sf, t_s0, *f_s)
                for h2 in range(2):
                    r = slice(64 * h2, 64 * h2 + 64)
                    c = slice(16 * h2, 16 * h2 + 16)
                    new = bs[r, 0:256].rearrange("p (a c) -> p a c", c=32)[:, :, c]
                    if t_sf is None:
                        t_s = dve.do(lambda e, r=r, c=c, new=new, s_new=s_new: e.tensor_copy(s_new[r, :, c], new),
                                     "state", ns=ve(128))
                    else:
                        t_s = dve.do(lambda e, r=r, c=c, new=new, s_new=s_new: e.tensor_tensor(
                            s_new[r, :, c], new, SF[r, :, c], ALU.add), "state", ns=ve(128))
                release(bs, t_s)
                t_sf_read = t_s
                done[("state", n)] = (s_new, t_s, k_s, None)
                done[("P2s", n)] = (t_xd, t_sf, t_b)
                if n % TPB:
                    yield from need(("s_read", n - 1))
                    r_St.free[k_old] = (done[("s_read", n - 1)], t_sf)

        def layernorm(t_mm, bk, resid, w_res, r, w_r, mark):
            k, s_, f_s = yield from r_st.take()
            yield from at(dve, t_mm, *w_res, *w_r)
            t0 = dve.do(lambda e: e.tensor_tensor(r, bk[:, 0:256], resid, ALU.add), "ln_add", ns=ve(256))
            release(bk, t0)
            yield from at(dve, t0, *f_s)
            t1 = dve.do(lambda e: e.bn_stats(s_[:, 0:6], r), "ln_stats", ns=ve(256))
            yield from at(dve, t1)
            t2 = dve.do(lambda e: e.bn_aggr(s_[:, 6:8], s_[:, 0:6]), "ln_aggr", ns=80)
            yield from at(pool, t2, t_cst)
            t3 = pool.do(lambda e: e.tensor_scalar(s_[:, 8:9], s_[:, 7:8], EPS, None, ALU.add), "ln_eps", ns=180)
            yield from at(pool, t3)
            t4 = pool.do(lambda e: e.tensor_tensor(s_[:, 9:10], s_[:, 8:9], mhalf[:, 0:1], ALU.pow), "ln_rstd", ns=470)
            yield from at(dve, t4)
            t5 = dve.do(lambda e: e.tensor_scalar(r, r, s_[:, 6:7], s_[:, 9:10], ALU.subtract, ALU.mult), mark,
                        ns=ve(256, True) + 120)
            r_st.free[k] = (t5,)
            return t0, t5

        def transpose2(src, w_src, dst, w_dst, mark):
            yield from at(pe, t_cst, *w_src)
            bk = yield from bank()
            for k in range(2):
                t = pe.do(lambda e, k=k: e.transpose(bk[:, 128 * k:128 * k + 128], src[:, 128 * k:128 * k + 128],
                          ident[:, :]), mark + "_pe", ns=60)
            yield from at(act, t, *w_dst)
            t2 = act.do(lambda e: e.copy(dst, bk[:, 0:256].rearrange("p (a b) -> p a b", a=2)), mark, ns=ac(256) - 90)
            release(bk, t2)
            return t, t2

        for dst, name in ((wout, "wout"), (pw, "pw"), (qw, "qw"), (w1, "w1"), (w2, "w2")):
            t_wo = load(dst[:, :, :], a[name], "ld_w")
        for dst, name in ((bo, "bo"), (bp, "bp"), (b2, "b2"), (qbc, "qb"), (b1c, "b1")):
            t_wb = load(dst[:, :], a[name], "ld_b")

        def p2x():
            for n in range(NT):
                k_xr, x_, f_x = yield from r_xr.take()
                yield from at(sp, *f_x)
                t_x = load(x_[:, :], a["x"][128 * n:128 * n + 128, :], f"ld_x{k_xr}")
                yield from at(pool, t_x, t_wb)
                t_x = pool.do(lambda e, x_=x_: e.tensor_tensor(x_[:, :], x_[:, :], bo[:, :], ALU.add), "x_bias", ns=690)
                done[("xr", n)] = (x_, t_x, k_xr)

        def p2c():
            for n in range(NT):
                g, i = divmod(n, GT)
                yield from need(("P2y", n), ("P2s", n))
                by, t_y = done[("P2y", n)]
                dc, k_dc = done[("P2a", n)][2], done[("P2a", n)][9]
                k_y, y, f_y = yield from r_y1.take()
                yield from at(dve, *t_y, *f_y)
                if n % TPB == 0:
                    t = dve.do(lambda e, y=y, by=by, i=i: e.tensor_tensor(y[:, :], by[:, 0:256], gt[:, i, :], ALU.mult),
                               "y_gate", ns=ve(256))
                    release(by, t)
                else:
                    t = dve.do(lambda e, y=y, by=by, dc=dc: e.tensor_tensor(
                        by_head(y[:, :]), by_head(by[:, 256:512]), per_head(dc[:, 0:16]), ALU.mult), "y_dec", ns=ve(256))
                    yield from at(dve, t)
                    t = dve.do(lambda e, y=y, by=by: e.tensor_tensor(y[:, :], by[:, 0:256], y[:, :], ALU.add), "y_sum",
                               ns=ve(256))
                    release(by, t)
                    yield from at(dve, t)
                    t = dve.do(lambda e, y=y, i=i: e.tensor_tensor(y[:, :], y[:, :], gt[:, i, :], ALU.mult), "y_gate",
                               ns=ve(256))
                t_s = done[("P2s", n)]
                r_dec.free[k_dc] = (t, *t_s[0:2])
                done[("P2", n)] = (t, *t_y, *t_s)
                k_t, yt, f_t = yield from r_yT.take()
                t_pe, t_t = yield from transpose2(y, (t,), yt[:, :, :], f_t, "yT")
                r_y1.free[k_y] = (t_pe,)
                yield from at(pe, t_t, t_wo)
                bk = yield from bank()
                for k in range(2):
                    t = pe.do(lambda e, k=k, bk=bk, yt=yt: e.matmul(bk[:, 0:256], yt[:, k, :], wout[:, k, :],
                              start=k == 0, stop=k == 1), "wout_mm", ns=mm(256))
                r_yT.free[k_t] = (t,)
                yield from need(("xr", n))
                x_, t_x, k_xr = done[("xr", n)]
                if n >= 4:
                    yield from need(("x1free", n - 4))
                w = (done[("x1free", n - 4)],) if n >= 4 else ()
                t0, t5 = yield from layernorm(t, bk, x_[:, :], (t_x,), x1[:, n % 4, :], w, "ln1")
                r_xr.free[k_xr] = (t0,)
                done[("x1", n)] = t5

        def p3q():
            for g in range(NG):
                w_t = (done[("q", g - 1)][0],) if g else ()
                for i in range(GT):
                    n = GT * g + i
                    yield from need(("x1", n))
                    x = x1[:, n % 4, :]
                    t_pe, t_t = yield from transpose2(x, (done[("x1", n)],), tT[:, :, 128 * i:128 * i + 128], w_t, "x1T")
                    yield from at(pool, t_pe, t_wb)
                    done[("x1b", n)] = pool.do(lambda e, x=x: e.tensor_tensor(x, x, bp[:, :], ALU.add), "x1b", ns=690)
                w_q = (done[("q", g - 1)][1],) if g else ()
                for m in range(2):
                    yield from at(pe, t_t, t_wo)
                    bk = yield from bank()
                    for k in range(2):
                        t = pe.do(lambda e, bk=bk, m=m, k=k: e.matmul(bk[:, 0:GW], qw[:, k, 128 * m:128 * m + 128],
                                  tT[:, k, :], start=k == 0, stop=k == 1), "q_mm", ns=mm(GW))
                    yield from at(act, t, t_wb, *w_q)
                    t1 = act.do(lambda e, bk=bk, m=m: e.activation(qhi[:, m, :].bitcast(R), bk[:, 0:GW], ACT.Identity,
                                bias=qbc[:, m:m + 1]), "q_hi", ns=ac(GW) + 90)
                    yield from at(dve, t1, *w_q)
                    t2 = dve.do(lambda e, bk=bk, m=m: e.scalar_tensor_tensor(
                        out=qf[:, m, :].bitcast(R), in0=bk[:, 0:GW], scalar=qbc[:, m:m + 1], in1=qhi[:, m, :],
                        op0=ALU.add, op1=ALU.subtract), "q_lo", ns=ve(GW))
                    release(bk, t1, t2)
                if g:
                    yield from need(("P3pe", g - 1))
                w = [done[("P3pe", g - 1)]] if g else [t_q1]
                yield from at(sp, t2, *w)
                done[("q", g)] = (t, stack(qhi, qf, qst, t1, t2, w, "q_stack"))

        def p3a(lane, lanes_):
            yield from need("kv")
            t_ks, t_vs, t_mr = done["kv"]
            for n in range(lane, NT, lanes_):
                g, i = divmod(n, GT)
                b = n // TPB
                yield from need(("q", g))
                if n:
                    yield from need(("a_start", n - 1))
                k_m, m_, f_m = yield from r_mx.take()
                k_p, pb, f_p = yield from r_P.take()
                done[("a_start", n)] = True
                for j in range(3):
                    n0, n1 = 3 * j, min(3 * j + 3, 8)
                    w = (n1 - n0) * 2
                    yield from at(pe, done[("q", g)][1], t_ks, t_mr)
                    bk = yield from bank()
                    for p in range(n0, n1):
                        t = pe.do(lambda e, p=p, n0=n0, bk=bk, i=i, b=b: e.matmul(
                            bk[:, 2 * S * (p - n0):2 * S * (p - n0 + 1)], qst[0:97, p, 128 * i:128 * i + 128],
                            kst[0:97, b, p, :], start=True, stop=True), "s_mm", ns=mmr(2 * S))
                    v = bk[:, 0:w * S].rearrange("p (h s) -> p h s", s=S)
                    yield from at(dve, t, *f_m)
                    t1 = dve.do(lambda e, v=v, m_=m_, n0=n0, w=w: e.tensor_reduce(m_[:, 2 * n0:2 * n0 + w], v, AX, ALU.max),
                                "s_max", ns=ve(S * w))
                    yield from at(dve, t1, *f_p)
                    t2 = dve.do(lambda e, v=v, m_=m_, n0=n0, w=w, pb=pb: e.tensor_tensor(
                        pb[:, 2 * S * n0:2 * S * n0 + w * S].rearrange("p (h s) -> p h s", s=S), v,
                        m_[:, 2 * n0:2 * n0 + w].unsqueeze(2).to_broadcast([128, w, S]), ALU.subtract),
                        "s_sub", ns=ve(S * w))
                    release(bk, t2)
                r_mx.free[k_m] = (t2,)
                done[("S", n)] = t
                if i == GT - 1:
                    yield from need(*((("S", m) for m in range(GT * g, n))))
                    done[("P3pe", g)] = t
                yield from exp_turn()
                yield from at(act, t2)
                t3 = act.do(lambda e, pb=pb: e.activation(pb[:, :], pb[:, :], ACT.Exp, scale=SCALE), "p_exp", ns=ac(HS))
                done[("P", n)] = (pb, t3, k_p)

        def p3b():
            for n in range(NT):
                b = n // TPB
                yield from need(("P", n))
                pb, t3, k_p = done[("P", n)]
                k_pt, pt, f_pt = yield from r_PT.take()
                tps = []
                for j in range(3):
                    m0, m1 = 4 * j, min(4 * j + 4, NBLK)
                    yield from at(pe, t3, t_cst)
                    bk = yield from bank()
                    for m in range(m0, m1):
                        w = blk_rows(m)
                        t = pe.do(lambda e, m=m, m0=m0, w=w, bk=bk, pb=pb: e.transpose(
                            bk[0:w, 128 * (m - m0):128 * (m - m0) + 128], pb[:, 128 * m:128 * m + w], ident[:, :]),
                            "pT_mm", ns=60)
                    if j < 2:
                        q = act if j == 0 else dve
                        yield from at(q, t, t_rbi, *f_pt)
                        t4 = q.do(lambda e, m0=m0, m1=m1, bk=bk, pt=pt, j=j: (e.tensor_copy if j else e.copy)(
                            pt[:, m0:m1, :], bk[:, :].rearrange("p (a b) -> p a b", b=128)), "pT_v" if j else "pT", ns=600)
                    else:
                        w = blk_rows(9)
                        yield from at(act, t, t_rbi, *f_pt)
                        act.do(lambda e, bk=bk, pt=pt: e.copy(pt[:, 8, :], bk[:, 0:128]), "pT", ns=200)
                        t4 = act.do(lambda e, bk=bk, pt=pt, w=w: e.copy(pt[0:w, 9, :], bk[0:w, 128:256]), "pT", ns=200)
                    tps.append(t4)
                    release(bk, t4)
                r_P.free[k_p] = (t,)
                yield from at(pe, *tps, done["kv"][1])
                bo_ = yield from bank()
                for m in range(NBLK):
                    w = blk_rows(m)
                    lo, hi = blk_heads(m)
                    nh = hi - lo + 1
                    t = pe.do(lambda e, m=m, w=w, lo=lo, nh=nh, bo_=bo_, pt=pt, b=b: e.matmul(
                        bo_[:, 17 * lo:17 * (lo + nh)], pt[0:w, m, :], vb[0:w, b, m, 0:17 * nh],
                        start=m == 0, stop=m == NBLK - 1, skip_group_check=True), "pv_mm", ns=mm(51))
                r_PT.free[k_pt] = (t,)
                k_r, rc_, f_rc = yield from r_rc.take()
                k_o, o_, f_o = yield from r_ob.take()
                ov = bo_[:, 0:272].rearrange("p (h c) -> p h c", c=17)
                yield from at(dve, t, *f_rc)
                t1 = dve.do(lambda e, ov=ov, rc_=rc_: e.reciprocal(rc_[:, :], ov[:, :, 16]), "p_rcp", ns=170)
                yield from at(dve, t1, *f_o)
                t2 = dve.do(lambda e, ov=ov, rc_=rc_, o_=o_: e.tensor_tensor(
                    o_[:, :].rearrange("p (h c) -> p h c", c=16), ov[:, :, 0:16],
                    rc_[:, :].unsqueeze(2).to_broadcast([128, 16, 16]), ALU.mult), "p_norm", ns=ve(256))
                r_rc.free[k_r] = (t2,)
                release(bo_, t2)
                done[("O", n)] = (o_, t2, k_o)

        def p3c():
            for n in range(NT):
                yield from need(("O", n))
                o_, t2, k_o = done[("O", n)]
                k_t, ot, f_t = yield from r_oT.take()
                t_pe, t_t = yield from transpose2(o_, (t2,), ot[:, :, :], f_t, "oT")
                r_ob.free[k_o] = (t_pe,)
                yield from at(pe, t_t, t_wo)
                bk = yield from bank()
                for k in range(2):
                    t = pe.do(lambda e, k=k, bk=bk, ot=ot: e.matmul(bk[:, 0:256], ot[:, k, :], pw[:, k, :],
                              start=k == 0, stop=k == 1), "proj_mm", ns=mm(256))
                r_oT.free[k_t] = (t,)
                if n >= FT:
                    yield from need(("x2free", n - FT))
                w = (done[("x2free", n - FT)],) if n >= FT else (done["kv"][1],)
                t0, t5 = yield from layernorm(t, bk, x1[:, n % 4, :], (done[("x1b", n)],), x2[:, n % FT, :], w, "ln2")
                done[("x1free", n)] = t0
                done[("x2", n)] = t5

        def p4a():
            t_f1 = None
            yield from need("kv")
            for g in range(NF):
                for i in range(FT):
                    n = FT * g + i
                    yield from need(("x2", n))
                    x = x2[:, i, :]
                    t_pe, t_t = yield from transpose2(x, (done[("x2", n)],), uT[:, :, 128 * i:128 * i + 128],
                                                      (t_f1, done["kv"][1]), "x2T")
                    yield from at(pool, t_pe, t_wb)
                    done[("x2b", n)] = pool.do(lambda e, x=x: e.tensor_tensor(x, x, b2[:, :], ALU.add), "x2b", ns=690)
                w = done["kv"][1:2]
                if g:
                    yield from need(("F2", FT * g - 1))
                    w = (done[("F2", FT * g - 1)],)
                t_r = []
                for m in range(8):
                    yield from at(pe, t_t, t_wo)
                    bk = yield from bank()
                    for k in range(2):
                        t_f1 = pe.do(lambda e, bk=bk, m=m, k=k: e.matmul(bk[:, :], w1[:, k, 128 * m:128 * m + 128],
                                     uT[:, k, :], start=k == 0, stop=k == 1), "ffn1_mm", ns=mm(512))
                    yield from at(act, t_f1, t_wb, *w)
                    t = act.do(lambda e, bk=bk, m=m: e.activation(hT[:, m, :], bk[:, :], ACT.Relu,
                               bias=b1c[:, m:m + 1]), "relu", ns=ac(512) + 90)
                    release(bk, t)
                    t_r.append(t)
                done[("h", g)] = t_r

        def p4b():
            for n in range(NT):
                g, i = divmod(n, FT)
                yield from need(("h", g))
                k_r, r, f_r = yield from r_res.take()
                for m in range(8):
                    if m % 4 == 0:
                        yield from at(pe, done[("h", g)][m + 3])
                    if m == 0:
                        bk = yield from bank()
                    t = pe.do(lambda e, bk=bk, m=m, i=i: e.matmul(bk[:, 0:256], hT[:, m, 128 * i:128 * i + 128],
                              w2[:, m, :], start=m == 0, stop=m == 7), "ffn2_mm", ns=mm(256))
                done[("F2", n)] = t
                t0, t5 = yield from layernorm(t, bk, x2[:, i, :], (done[("x2b", n)],), r[:, :], f_r, "ln3")
                done[("x2free", n)] = t0
                yield from at(sp, t5)
                t = sp.do(lambda e, n=n, r=r: e.dma_start(out[128 * n:128 * n + 128, :], r[:, :]), f"store{k_r}", 16)
                r_res.free[k_r] = (t,)
                stores.append(t)

        stores = []
        interleave([p_load(), p_kv(), p1(), p2a(), p2s(), p2y(), p2g(0, 3), p2g(1, 3), p2g(2, 3), p2x(), p2c(), p3q(),
                    p3b(), p3c(), p3a(0, 2), p3a(1, 2), p4a(), p4b()], (pe, act, dve, pool, sp))
        sp.wait(*stores)

        block = ctx.enter_context(nc.Block())

        @block.sync
        def _(eng):
            sp.run(eng)

        @block.tensor
        def _(eng):
            pe.run(eng)

        @block.vector
        def _(eng):
            dve.run(eng)

        @block.scalar
        def _(eng):
            act.run(eng)

        @block.gpsimd
        def _(eng):
            pool.run(eng)


def stacked_weights(W_XBC, b_XBC, W_gate, b_gate, W_logA, b_logA):
    w = np.zeros((KX, WCOLS), W_XBC.dtype)

    def put(col, h, rows, bias):
        r = 16 * (h % 2)
        for k in range(3):
            w[32 * k + r:32 * k + r + 16, col:col + rows.shape[0]] = rows.T
        w[96:98, col:col + rows.shape[0]] = bias

    for h in range(H):
        p, h2 = divmod(h, 2)
        put(128 * p + 64 * h2, h, W_XBC[h, 16:80], b_XBC[h, 16:80])
        put(1024 + 128 * p + 64 * h2, h, W_XBC[h, 80:144], b_XBC[h, 80:144])
        t = 2048 + WT * p
        put(t + 16 * h2, h, W_XBC[h, 0:16], b_XBC[h, 0:16])
        put(t + 32 + 16 * h2, h, W_gate[h], b_gate[h])
        put(t + 64 + h2, h, W_logA[h], b_logA[h])
    return w


def kernel(x, ctx_1024, mask_BxS2_bk0, L0_attn_W_logA, L0_attn_b_logA, L0_attn_W_XBC, L0_attn_b_XBC,
           L0_attn_W_gate, L0_attn_b_gate, L0_attn_W_out, L0_attn_b_out, L0_xattn_q_w, L0_xattn_q_b,
           L0_xattn_kv_w, L0_xattn_kv_b, L0_xattn_proj_w, L0_xattn_proj_b, L0_ffn_W1, L0_ffn_b1,
           L0_ffn_W2, L0_ffn_b2):
    import concourse.bacc as _bacc
    from concourse.bass_utils import run_bass_kernel_spmd as _run

    f = np.float32
    A = np.asarray

    def kmajor(w):
        w = A(w)
        return w.reshape(-1, 128, w.shape[1]).transpose(1, 0, 2)

    def col(v):
        return A(v).reshape(-1, 128).T

    def rows(v, n):
        return np.broadcast_to(A(v), (n, A(v).shape[0]))

    xf = A(x).reshape(B * T, D)
    kvb = A(L0_xattn_kv_b)
    mask = A(mask_BxS2_bk0)
    idx = np.arange(128)
    tri = (idx[:, None] <= idx[None, :]).astype(f)
    dl = np.zeros((66, 128), f)
    dl[64:66] = 1.0
    rb = np.zeros((66, 16, 128), f)
    for h in range(16):
        rb[h, h] = -1.0
        rb[32 + h, h] = -1.0
    negm = np.zeros((128, 1), f)
    negm[64:97] = -1.0
    arrays = {
        "x": xf,
        "xT": xf.T.reshape(2, 128, B * T).transpose(1, 0, 2),
        "wst": stacked_weights(A(L0_attn_W_XBC), A(L0_attn_b_XBC), A(L0_attn_W_gate), A(L0_attn_b_gate),
                               A(L0_attn_W_logA), A(L0_attn_b_logA)),
        "negm": negm, "dl": dl, "rb": rb.reshape(66, 2048),
        "ident": np.eye(128, dtype=f), "tri": tri,
        "sup": (idx[:, None] > idx[None, :]).astype(f), "ones": np.ones((128, 128), f),
        "mhalf": np.full((128, 1), -0.5, f),
        "wout": kmajor(A(L0_attn_W_out).T), "pw": kmajor(L0_xattn_proj_w), "qw": kmajor(L0_xattn_q_w),
        "kvw": kmajor(L0_xattn_kv_w), "w1": kmajor(L0_ffn_W1), "w2": kmajor(L0_ffn_W2),
        "b1": col(L0_ffn_b1), "qb": col(L0_xattn_q_b), "kb": col(kvb[0:256]),
        "bo": rows(L0_attn_b_out, 128), "bp": rows(L0_xattn_proj_b, 128), "b2": rows(L0_ffn_b2, 128),
        "bv": rows(kvb[256:512], S),
        "ctxT": A(ctx_1024).reshape(B * S, D).T.reshape(2, 128, B * S).transpose(1, 0, 2),
        "mcol": mask.T, "mrow": mask.reshape(1, B * S),
    }
    nc = _bacc.Bacc("TRN2", target_bir_lowering=False, num_devices=1)
    maps, aps = {}, {}
    for name, v in arrays.items():
        v = np.ascontiguousarray(v)
        maps[f"in_{name}"] = v
        aps[name] = nc.dram_tensor(f"in_{name}", v.shape, mybir.dt.from_np(v.dtype), kind="ExternalInput").ap()
    out = nc.dram_tensor("out_0", (B * T, D), F, kind="ExternalOutput").ap()
    build(nc, aps, out)
    r = _run(nc, [maps], core_ids=[0])
    return r.results[0]["out_0"].reshape(B, T, D)
```

```python
from contextlib import ExitStack

import numpy as np

import concourse.bass as bass
from concourse import mybir

F = mybir.dt.float32
R = mybir.dt.float32r
U8 = mybir.dt.uint8
ALU = mybir.AluOpType
ACT = mybir.ActivationFunctionType
AX = mybir.AxisListType.X

B, T, D, H, S = 4, 1024, 256, 16, 77
NT = B * T // 128
GT = 2
NG = NT // GT
TPB = T // 128
KX = 98
WT = 162
WC = 8 * WT
WCOLS = WC + 1024
NEG = -1.0e30
EPS = 1e-5
SCALE = 0.25
HS = H * S
NBLK = 10
FT = 2
NF = NT // FT
X1N = 4
X2N = 4
GW = 128 * GT


def by_head(ap):
    return ap.rearrange("p (m r c) -> p m r c", r=2, c=16)


def per_head(ap):
    return ap.rearrange("p (r m) -> p m r", r=2).unsqueeze(3).to_broadcast([128, 8, 2, 16])


def heads(q):
    return [8 * (q % 2) + q // 2 + 2 * k for k in range(4)]


def blk_rows(m):
    return min(128, HS - 128 * m)


PV = [(4 * a + q, 2 * S * (4 * a + q) // 128 + k, k == 0, 2 * S * (4 * a + q) // 128 + k == (2 * S * (4 * a + q + 1) - 1) // 128)
      for a in range(2) for k in range(3) for q in range(4)
      if 2 * S * (4 * a + q) // 128 + k <= (2 * S * (4 * a + q + 1) - 1) // 128]


class Token:

    def __init__(self, sem, val, at=0.0):
        self.sem, self.val, self.at = sem, val, at


class Marks:

    def __init__(self, make):
        self.make, self.sems, self.vals, self.last = make, {}, {}, {}

    def bump(self, name, by, at):
        if name not in self.sems:
            self.sems[name] = self.make("s_" + name)
            self.vals[name] = 0
        self.vals[name] += by
        self.last[name] = Token(name, self.vals[name], at)
        return self.last[name]


TABLE = {"bc_silu": "silu", "tokb_silu": "silu", "tok_silu": "silu", "dec": "exp", "decay_exp": "exp", "ec": "exp",
         "p_exp": "exp"}
WARM = 200e3


class Queue:

    def __init__(self, marks, latency, slow=1.0):
        self.marks, self.items, self.seen, self.now, self.latency = marks, [], {}, 0.0, latency
        self.slow, self.table = slow, None

    def start(self, tokens):
        return max([self.now] + [t.at + self.latency for t in tokens if t is not None])

    def wait(self, *tokens):
        self.now = self.start(tokens)
        need = {}
        for t in tokens:
            if t is not None:
                need[t.sem] = max(need.get(t.sem, 0), t.val)
        for name, val in need.items():
            if self.seen.get(name, 0) < val:
                self.seen[name] = val
                self.items.append(("wait", name, val))

    def do(self, fn, mark=None, by=1, ns=0.0):
        if by == 16:
            self.now += 625.0
            token = self.marks.bump(mark, by, self.now + 1900.0 + ns)
        else:
            self.now += ns * (self.slow if self.now < WARM else 1.0)
            if mark in TABLE and TABLE[mark] != self.table:
                self.now += 1283.0
                self.table = TABLE[mark]
            token = self.marks.bump(mark, by, self.now) if mark else None
        self.items.append(("do", fn, mark, by))
        return token

    def run(self, eng):
        for it in self.items:
            if it[0] == "wait":
                eng.wait_ge(self.marks.sems[it[1]], it[2])
            else:
                ins = it[1](eng)
                if it[2]:
                    ins.then_inc(self.marks.sems[it[2]], it[3])


def at(queue, *tokens):
    yield queue, tokens
    queue.wait(*tokens)


BLOCKED = (None, ())


def interleave(lanes, queues):
    state = {ln: next(ln) for ln in lanes}
    idle = 0
    while lanes:
        for ln in list(lanes):
            if state[ln][0] is None:
                try:
                    state[ln] = next(ln)
                except StopIteration:
                    lanes.remove(ln)
        best, when = None, 0.0
        for ln in lanes:
            q, toks = state[ln]
            if q is not None:
                t = q.start(toks)
                if best is None or t < when:
                    best, when = ln, t
        if best is None:
            idle += 1
            assert idle < 100, "no lane can go on"
            continue
        idle = 0
        try:
            state[best] = next(best)
        except StopIteration:
            lanes.remove(best)


class Ring:

    def __init__(self, bufs, first=()):
        self.bufs, self.free, self.n = bufs, [first] * len(bufs), 0

    def take(self):
        i = self.n % len(self.bufs)
        while self.free[i] is None:
            yield BLOCKED
            i = self.n % len(self.bufs)
        self.n += 1
        was, self.free[i] = self.free[i], None
        return i, self.bufs[i], was


def mm(n):
    return max(220, n / 0.6)


def mmr(n):
    return max(90, n / 2.4)


def mmc(n):
    return n / 2.4 + 40


def ac(n):
    return 52 + n / 1.2


def ve(n, fast=False):
    return 70 + n / (1.92 if fast else 0.96)


def build(nc, a, out):
    ctx = ExitStack()
    with ctx:
        def sb(name, shape, dt=F):
            return ctx.enter_context(nc.sbuf_tensor(name, shape, dt))

        marks = Marks(lambda n: ctx.enter_context(nc.semaphore(n)))
        pe, act, dve, pool, sp = (Queue(marks, *c) for c in ((270.0, 1.8), (170.0,), (180.0,), (180.0,), (100.0,)))

        banks = [ctx.enter_context(nc.psum_tensor(f"bank{i}", [128, 512], F)) for i in range(8)]
        free_banks = [(b, ()) for b in banks]

        def bank():
            while not free_banks:
                yield BLOCKED
            free_banks.sort(key=lambda f: pe.start(f[1]))
            b, toks = free_banks.pop(0)
            pe.wait(*toks)
            return b

        def release(b, *toks):
            free_banks.append((b, toks))

        wst = sb("wst", [KX, WCOLS], R)
        hT = sb("hT", [128, 8, 128 * FT])
        wraw1 = hT[0:KX, :, :].rearrange("p a b -> p (a b)")
        ident = sb("ident", [128, 128])
        tri = sb("tri", [128, 128])
        sup = sb("sup", [128, 128])
        negm = sb("negm", [128, 1])
        wg = sb("wg", [32, 256])
        gbc = sb("gbc", [128, 2])
        wout = sb("wout", [128, 2, 256])
        qw = sb("qw", [128, 2, 256])
        pw = sb("pw", [128, 2, 256])
        w1h = sb("w1h", [128, 2, 1024], R)
        w1l = sb("w1l", [128, 2, 1024], R)
        w2 = sb("w2", [128, 8, 256])
        b1c = sb("b1c", [128, 8])
        qbc = sb("qbc", [128, 2])
        kbc = sb("kbc", [128, 2])
        bo = sb("bo", [128, 256])
        bp = sb("bp", [128, 256])
        b2 = sb("b2", [128, 256])
        mhalf = sb("mhalf", [128, 1])

        P = [sb(f"P{i}", [128, HS]) for i in range(2)]
        PT = [sb(f"PT{i}", [128, NBLK, 128]) for i in range(1)]
        kvw = PT[0][:, 0:8, :].rearrange("p a b -> p (a b)").rearrange("p (a b) -> p a b", a=2)
        x2s = sb("x2s", [128, X2N, 256])
        x2 = x2s
        uh = sb("uh", [128, 2, 128 * FT], R)
        ul = sb("ul", [128, 2, 128 * FT], R)
        wraw2 = P[1][0:KX, 0:WCOLS - 2048]
        ctxT = P[0][:, 0:2 * B * S].rearrange("p (a s) -> p a s", a=2)
        kT = P[0][:, 2 * B * S:4 * B * S].rearrange("p (a s) -> p a s", a=2)
        bv = P[1][0:S, 2 * B * S:2 * B * S + 256]
        khi = P[1][:, 0:2 * B * S].rearrange("p (a s) -> p a s", a=2)
        vt = x2s[0:S, :, :].rearrange("p a b -> p (a b)")[:, 0:B * 256].rearrange("p (b h c) -> p b h c", b=B, h=H)
        kst = sb("kst", [97, B, 8, 2 * S], R)
        mrow = sb("mrow", [97, B * S], U8)
        mcol = sb("mcol", [S, B], U8)
        valid = sb("valid", [S, B])
        vb = sb("vb", [128, B, len(PV), 32])
        nval = sb("nval", [S, B])

        xraw = sb("xraw", [96, 8, GW])
        negl = sb("negl", [32, 1])
        xst = sb("xst", [KX, 8, GW], R)
        qf = sb("qf", [128, 2, GW])
        qhi = sb("qhi", [128, 2, GW])
        qst = sb("qst", [97, 8, GW], R)
        Bc = sb("Bc", [128, 8, GW])
        Cc = sb("Cc", [128, 8, GW])
        Bt = [sb(f"Bt{i}", [128, 1024]) for i in range(2)]
        Xt = sb("Xt", [128, 2 * GT, 8, 48])
        gT = sb("gT", [128, 2, 2, GW])
        ind = sb("ind", [32, 256], R)
        ec = [sb(f"ec{i}", [128, 256]) for i in range(2)]
        la = sb("la", [128, 2 * GT, 2, 16])
        DL = [sb(f"DL{i}", [34, 128], R) for i in range(2)]
        RB = sb("RB", [34, 2048], R)
        dec = [sb(f"dec{i}", [128, 16]) for i in range(2)]
        E = [sb(f"E{i}", [128, 4, 128]) for i in range(4)]
        Xd = [sb(f"Xd{i}", [128, 256]) for i in range(2)]
        St = [sb(f"St{i}", [128, 8, 32]) for i in range(2)]
        ST = sb("ST", [128, 2, 128])
        xr = [sb(f"xr{i}", [128, 256]) for i in range(2)]
        yT = [sb(f"yT{i}", [128, 256]) for i in range(2)]
        x1 = sb("x1", [128, X1N, 256])
        tT = sb("tT", [128, 2, GW])
        mx = [sb(f"mx{i}", [128, 16]) for i in range(2)]
        rc = [sb(f"rc{i}", [128, 16]) for i in range(2)]
        oT = [sb(f"oT{i}", [128, 2, 128]) for i in range(2)]
        res = [sb(f"res{i}", [128, 256]) for i in range(2)]
        one_s = res[0][0:S, 0:S]
        st = [sb(f"st{i}", [128, 10]) for i in range(6)]

        done = {}

        def need(*keys):
            while any(k not in done for k in keys):
                yield BLOCKED

        r_DL, r_dec, r_E, r_Xd, r_St = Ring(DL), Ring(dec), Ring(E), Ring(Xd), Ring(St)
        r_xr, r_ec, r_yT, r_mx, r_P, r_PT = Ring(xr), Ring(ec), Ring(yT), Ring(mx), Ring(P), Ring(PT)
        r_rc, r_oT, r_res, r_st, r_Bt = Ring(rc), Ring(oT), Ring(res), Ring(st), Ring(Bt)
        silu = [False]

        def exp_turn():
            while silu[0]:
                yield BLOCKED

        def load(dst, src, mark, ns=0.0):
            return sp.do(lambda e: e.dma_start(dst, src), mark, 16, ns)

        dlr = PT[0][0:34, 8, :]
        rbr = PT[0][0:34, :, :].rearrange("p a b -> p (a b)")
        indr = E[0][0:32, 0:2, :].rearrange("p a b -> p (a b)")
        rbr2 = x2s[0:34, :, :].rearrange("p a b -> p (a b)")
        load(wraw1, a["wst"][:, 0:2048], "ld_wst", ns=2400)
        load(wraw2, a["wst"][:, 2048:WCOLS], "ld_wst", ns=2400)
        t_w = load(negm[:, :], a["negm"], "ld_wst", ns=2400)
        t_x0 = load(xraw[:, :, :], a["x3"][:, :, 0:GW], "ld_x3", ns=3000)
        load(wg[:, :], a["wg"], "ld_gate")
        load(gbc[:, :], a["gb"], "ld_gate")
        t_ng = load(negl[:, :], a["negl"], "ld_gate")
        for dst, name in ((tri, "tri"), (sup, "sup"), (ident, "ident"), (mhalf, "mhalf")):
            t_cst = load(dst[:, :], a[name], "ld_cst")
        load(dlr, a["dl"], "ld_rb")
        load(rbr[:, 0:1024], a["rb"][:, 0:1024], "ld_rb")
        load(rbr2[:, 0:1024], a["rb"][:, 1024:2048], "ld_rb")
        t_rb = load(indr, a["ind"], "ld_rb")

        t_x1 = dve.do(lambda e: e.memset(xst[96:98, :, :].bitcast(F), 1.0), "ones_rows", ns=1300)
        t_q1 = dve.do(lambda e: e.memset(qst[96:97, :, :].bitcast(F), 1.0), "ones_rows", ns=1300)
        t_xz = dve.do(lambda e: e.memset(Xt[:, :, :, :], 0.0), "ones_rows", ns=1500)

        dve.wait(t_w)
        for c, w in ((slice(0, 2048), wraw1), (slice(2048, WCOLS), wraw2)):
            t = dve.do(lambda e, c=c, w=w: e.tensor_copy(wst[:, c], w), "wst_hi", ns=670)
            dve.wait(t)
            t_wst = dve.do(lambda e, c=c, w=w: e.scalar_tensor_tensor(
                out=wst[64:KX, c], in0=wst[64:KX, c].bitcast(F), scalar=negm[64:KX, 0:1], in1=w[64:KX, :],
                op0=ALU.mult, op1=ALU.add), "wst_lo", ns=1340)
        t_dli = Token("dl_init", 2)
        for i in range(2):
            t_s0 = pool.do(lambda e, i=i: e.memset(St[i][:, :, :], 0.0), "s_zero")
        t_kz = pool.do(lambda e: e.memset(kst[:, :, :, :].bitcast(F), 0.0), "kv_zero")
        t_vz = pool.do(lambda e: e.memset(vb[:, :, :, :], 0.0), "kv_zero")

        def p_init():
            yield from at(dve, t_rb)
            for i in range(2):
                dve.do(lambda e, i=i: e.tensor_copy(DL[i][:, :], dlr), "dl_init", ns=140)
            for j, src in enumerate((rbr, rbr2)):
                t = dve.do(lambda e, j=j, src=src: e.tensor_copy(RB[:, 1024 * j:1024 * j + 1024], src[:, 0:1024]),
                           "rb_init", ns=600)
                yield from at(dve)
            done["init"] = (t, dve.do(lambda e: e.tensor_copy(ind[:, :], indr), "ind_r", ns=200))

        def p_weights():
            yield from at(sp)
            for dst, name in ((wout, "wout"), (pw, "pw"), (qw, "qw"), (w2, "w2")):
                yield from at(sp)
                t = load(dst[:, :, :], a[name], "ld_w", ns=3000)
            yield from at(sp, t_wst)
            raw = hT[:, :, :].rearrange("p a b -> p (a b)").rearrange("p (a b) -> p a b", a=2)
            t_w1 = load(raw, a["w1"], "ld_w1", ns=3000)
            for dst, name in ((bo, "bo"), (bp, "bp"), (b2, "b2"), (qbc, "qb"), (b1c, "b1")):
                yield from at(sp)
                t2 = load(dst[:, :], a[name], "ld_b", ns=1500)
            for k in range(2):
                yield from at(dve, t_w1)
                t = dve.do(lambda e, k=k: e.tensor_copy(w1h[:, k, :], raw[:, k, :]), "w1_hi", ns=600)
                yield from at(dve, t)
                t = dve.do(lambda e, k=k: e.tensor_tensor(w1l[:, k, :], raw[:, k, :], w1h[:, k, :].bitcast(F),
                           ALU.subtract), "w1_lo", ns=1150)
            done["w1"] = t
            
        def stack(hi, lo, dst, t_hi, t_lo, waits, mark):
            tok = None
            for src, row in ((hi, 0), (hi, 64), (lo, 32)):
                for q in range(4):
                    yield from at(sp, t_hi, *waits, *((t_lo,) if row == 32 else ()))
                    d = dst[row:row + 32, q:8:4, :].bitcast(F)
                    s = src[32 * q:32 * q + 32, :, :]
                    tok = sp.do(lambda e, d=d, s=s: e.dma_start(d, s), mark, 16)
            return tok

        def p_load():
            t_lo = None
            for g in range(NG):
                t0, w = t_x0, t_x1
                if g:
                    yield from need(("P1pe", g - 1))
                    w = done[("P1pe", g - 1)]
                    yield from at(sp, w, t_lo)
                    t0 = load(xraw[:, :, :], a["x3"][:, :, GW * g:GW * g + GW], "ld_x3", ns=2000)
                for j in range(2):
                    c = slice(4 * j, 4 * j + 4)
                    yield from at(act, t0, w)
                    t_hi = act.do(lambda e, c=c: e.copy(xst[0:96, c, :], xraw[:, c, :]), "x_hi", ns=ac(4 * GW))
                    yield from at(dve, t_hi)
                    t_lo = dve.do(lambda e, c=c: e.tensor_tensor(
                        xst[32:64, c, :], xraw[32:64, c, :], xst[32:64, c, :].bitcast(F), ALU.subtract), "x_lo",
                        ns=ve(4 * GW))
                done[("xst", g)] = t_lo

        def p_kv():
            sp_l = [(kvw, "kvw"), (ctxT, "ctxT"), (kbc[:, :], "kb"), (bv[:, :], "bv"),
                    (mcol[:, :], "mcol"), (mrow[96:97, :], "mrow")]
            yield from need("init")
            t_rbi = done["init"][0]
            t_v1 = dve.do(lambda e: e.memset(one_s, 1.0), "kv_one", ns=100)
            for dst, name in sp_l:
                yield from at(sp, t_rbi)
                t_l = load(dst, a[name], "ld_kv", ns=1500)
            yield from at(dve, t_l)
            t_va = dve.do(lambda e: e.tensor_scalar(valid[:, :], mcol[:, :], -1.0, 1.0, ALU.mult, ALU.add), "valid",
                          ns=100)
            for b in range(B):
                yield from at(dve, t_kz)
                t_mr = dve.do(lambda e, b=b: e.tensor_scalar(
                    kst[96:97, b, :, :].rearrange("p a (h s) -> p (a h) s", s=S),
                    mrow[96:97, b * S:(b + 1) * S].unsqueeze(1).to_broadcast([1, H, S]), NEG, None, ALU.mult), "mask_row",
                    ns=710)
            yield from at(pe, t_v1, t_va)
            bk = yield from bank()
            t = pe.do(lambda e, bk=bk: e.matmul(bk[0:S, 0:B], one_s, valid[:, :], start=True, stop=True), "n_valid",
                      ns=220)
            yield from at(dve, t)
            t = dve.do(lambda e, bk=bk: e.reciprocal(nval[:, :], bk[0:S, 0:B]), "v_norm", ns=100)
            yield from at(dve, t)
            t = dve.do(lambda e, bk=bk: e.tensor_tensor(nval[:, :], bk[0:S, 0:B], nval[:, :], ALU.mult), "v_norm", ns=100)
            release(bk, t)
            yield from at(dve, t)
            t_va = dve.do(lambda e: e.tensor_tensor(valid[:, :], valid[:, :], nval[:, :], ALU.mult), "v_norm", ns=100)
            tks = []
            for m in range(2):
                yield from at(pe, t_l)
                bk = yield from bank()
                for k in range(2):
                    t = pe.do(lambda e, bk=bk, m=m, k=k: e.matmul(bk[:, 0:B * S], kvw[:, k, 128 * m:128 * m + 128],
                              ctxT[:, k, :], start=k == 0, stop=k == 1), "k_mm" if k else None, ns=mm(308))
                yield from at(act, t, t_l)
                t = act.do(lambda e, bk=bk, m=m: e.activation(kT[:, m, :], bk[:, 0:B * S], ACT.Identity,
                           bias=kbc[:, m:m + 1]), "k_bias", ns=400)
                release(bk, t)
                tks.append(t)
            yield from at(pool, *tks)
            t1 = pool.do(lambda e: e.tensor_copy(khi.bitcast(R), kT), "k_hi", ns=2200)
            yield from at(pool, t1)
            t2 = pool.do(lambda e: e.tensor_tensor(kT.bitcast(R), kT, khi, ALU.subtract), "k_lo", ns=1450)
            for src, row in ((khi, 0), (khi, 32), (kT, 64)):
                for q in range(4):
                    for h2 in range(2):
                        for m in range(2):
                            yield from at(sp, t1, t_kz, *((t2,) if row == 64 else ()))
                            d = kst[row + 16 * h2:row + 16 * h2 + 16, :, 4 * m + q, S * h2:S * h2 + S].bitcast(F)
                            s = src[32 * q + 16 * h2:32 * q + 16 * h2 + 16, m, :].rearrange("p (b s) -> p b s", s=S)
                            t_ks = sp.do(lambda e, d=d, s=s: e.dma_start(d, s), "k_stack", 16)
            for b in range(B):
                yield from at(pe)
                bk = yield from bank()
                for k in range(2):
                    t = pe.do(lambda e, bk=bk, b=b, k=k: e.matmul(bk[0:S, 0:256], ctxT[:, k, b * S:(b + 1) * S],
                              kvw[:, k, 256:512], start=k == 0, stop=k == 1), "v_mm" if k else None, ns=mm(256))
                yield from at(dve, t, t_v1)
                t = dve.do(lambda e, bk=bk, b=b: e.tensor_tensor(
                    vt[:, b, :, :], bk[0:S, 0:256].rearrange("p (h c) -> p h c", c=16),
                    bv[:, :].rearrange("p (h c) -> p h c", c=16), ALU.add), "v_bias", ns=340)
                release(bk, t)
                yield from at(dve, t, t_va)
                t = dve.do(lambda e, b=b: e.tensor_scalar(vt[:, b, :, :], vt[:, b, :, :], valid[:, b:b + 1], None,
                           ALU.mult), "v_ready", ns=300)
            for j, (p, m, _, _) in enumerate(PV):
                for r in range(2):
                    h = 2 * p + r
                    r0, r1 = max(S * h, 128 * m), min(S * h + S, 128 * m + blk_rows(m))
                    if r0 < r1:
                        d = vb[r0 - 128 * m:r1 - 128 * m, :, j, 16 * r:16 * r + 16]
                        s = vt[r0 - S * h:r1 - S * h, :, h, :]
                        yield from at(sp, t, t_vz)
                        t_vs = sp.do(lambda e, d=d, s=s: e.dma_start(d, s), "v_stack", 16)
            done["kv"] = (t_ks, t_vs, t_mr)

        def p1():
            for g in range(NG):
                yield from need(("xst", g))
                w_free, w_c = (), ()
                if g > 1:
                    ns = range(GT * (g - 2), GT * (g - 1))
                    yield from need(*(("P2", n) for n in ns))
                    w_free = tuple(t for n in ns for t in done[("P2", n)])
                if g:
                    ns = range(GT * (g - 1), GT * g)
                    yield from need(*(("C", n) for n in ns), *(("G", n, q) for n in ns for q in range(4)))
                    w_c = tuple(t for n in ns for t in (done[("C", n)], *(done[("G", n, q)] for q in range(4))))
                bts = []
                for i in range(GT):
                    bts.append((yield from r_Bt.take()))
                for i in range(GT):
                    _, bt, f_bt = bts[i]
                    x4 = (GT * g + i) % (2 * GT)
                    for b3 in range(3):
                        p0, p1_ = 3 * b3, min(3 * b3 + 3, 8)
                        yield from at(pe, done[("xst", g)], t_wst)
                        bx = yield from bank()
                        for p in range(p0, p1_):
                            t = pe.do(lambda e, p=p, p0=p0, i=i, bx=bx: e.matmul(
                                bx[:, WT * (p - p0):WT * (p - p0) + WT], xst[0:KX, p, 128 * i:128 * i + 128],
                                wst[0:KX, WT * p:WT * p + WT], start=True, stop=True),
                                "tok_mm" if p == p1_ - 1 else None, ns=mmr(WT))
                        v = bx[:, 0:WT * (p1_ - p0)].rearrange("p (a c) -> p a c", c=WT)
                        silu[0] = True
                        yield from at(act, t, t_xz, *w_free, *f_bt)
                        act.do(lambda e, v=v, bt=bt, p0=p0, p1_=p1_: e.activation(
                            bt[:, 128 * p0:128 * p1_].rearrange("p (a c) -> p a c", c=128), v[:, :, 0:128], ACT.Silu),
                            "tokb_silu", ns=ac(340))
                        t1 = act.do(lambda e, v=v, x4=x4, p0=p0, p1_=p1_: e.activation(
                            Xt[:, x4, p0:p1_, :].rearrange("p a (k c) -> p a k c", c=16)[:, :, 0:3:2, :],
                            v[:, :, 128:160].rearrange("p a (r c) -> p a r c", c=16), ACT.Silu), "tok_silu", ns=ac(85))
                        yield from at(dve, t, t1, *w_free)
                        t2 = dve.do(lambda e, v=v, x4=x4, p0=p0, p1_=p1_: e.tensor_copy(
                            la[:, x4, :, :].rearrange("p c (r m) -> p c r m", r=2)[:, :, :, p0:p1_],
                            v[:, :, 160:162].rearrange("p a r -> p r a").unsqueeze(1).to_broadcast(
                                [128, 2, 2, p1_ - p0])), "la_cp", ns=80)
                        release(bx, t1, t2)
                    done[("P1t", GT * g + i)] = (t1, t2)
                    bts[i] = (bts[i][0], bt, t1)
                done[("Bt", g)] = bts
                for n in range(0, 16, 2):
                    p, dst = n % 8, (Bc if n < 8 else Cc)
                    yield from at(pe, done[("xst", g)], t_wst)
                    bk = yield from bank()
                    for j in range(2):
                        c = WT * (p + j) if n < 8 else WC + 128 * (p + j)
                        t_pe = pe.do(lambda e, bk=bk, c=c, p=p + j, j=j: e.matmul(
                            bk[:, GW * j:GW * j + GW], wst[0:KX, c:c + 128], xst[0:KX, p, :], start=True, stop=True),
                            "bc_mm" if j else None, ns=mmr(GW))
                    yield from at(act, t_pe, *w_c)
                    t_bc = act.do(lambda e, bk=bk, p=p, dst=dst: e.activation(
                        dst[:, p:p + 2, :], bk[:, :].rearrange("p (a b) -> p a b", a=2), ACT.Silu), "bc_silu", ns=ac(512))
                    if n == 14:
                        silu[0] = False
                    release(bk, t_bc)
                done[("P1", g)] = (t_bc,)
                yield from at(pe, t_ng)
                bk = yield from bank()
                for p in range(8):
                    t_pe = pe.do(lambda e, bk=bk, p=p: e.matmul(
                        bk[32 * (p % 4):32 * (p % 4) + 32, GW * (p // 4):GW * (p // 4) + GW],
                        wg[:, 32 * p:32 * p + 32], xraw[0:32, p, :], start=True, stop=True, skip_group_check=True),
                        "gate_mm" if p == 7 else None, ns=mmc(GW))
                done[("P1pe", g)] = t_pe
                yield from at(dve, t_pe, *w_free)
                for m in range(2):
                    t3 = dve.do(lambda e, bk=bk, m=m, g=g: e.tensor_scalar(
                        gT[:, g % 2, m, :], bk[:, GW * m:GW * m + GW], gbc[:, m:m + 1], None, ALU.add), "gate_cp", ns=196)
                release(bk, t3)
                done[("gate", g)] = t3

        def p2a():
            for n in range(NT):
                g, i = divmod(n, GT)
                yield from need(("P1t", n), "init")
                t_rbi, t_ind = done["init"]
                k_dl, dl, f_dl = yield from r_DL.take()
                k_dc, dc, f_dc = yield from r_dec.take()
                yield from at(pe, *done[("P1t", n)], t_cst)
                bk = yield from bank()
                x4 = n % (2 * GT)
                l, l2 = la[:, x4, 0, :], la[:, x4, :, :].rearrange("p a b -> p (a b)")
                if n % TPB < TPB - 1:
                    pe.do(lambda e, l=l, bk=bk: e.matmul(bk[:, 0:16], sup[:, :], l, start=True, stop=True), ns=mm(16))
                t = pe.do(lambda e, l2=l2, bk=bk: e.matmul(bk[0:32, 64:192], l2, tri[:, :], start=True, stop=True),
                          "cum_mm", ns=mm(128))
                yield from at(act, t, t_dli, *f_dl)
                t1 = act.do(lambda e, dl=dl, bk=bk: e.copy(dl[0:32, :], bk[0:32, 64:192]), "cum_hi", ns=ac(128))
                yield from at(dve, t1, t_dli, t_ng, *f_dl)
                t3 = dve.do(lambda e, dl=dl, bk=bk: e.scalar_tensor_tensor(
                    out=dl[0:32, :], in0=dl[0:32, :].bitcast(F), scalar=negl[:, 0:1], in1=bk[0:32, 64:192],
                    op0=ALU.mult, op1=ALU.add), "cum_lo", ns=ve(128) + 60)
                done[("cum", n)] = (dl, t1, t3)
                t2 = t1
                if n % TPB < TPB - 1:
                    yield from exp_turn()
                    yield from at(act, t, t3, *f_dc)
                    t2 = act.do(lambda e, dc=dc, bk=bk: e.activation(dc[:, :], bk[:, 0:16], ACT.Exp), "dec", ns=64)
                if n % TPB == 0:
                    release(bk, t2, t3)
                done[("P2a", n)] = (dl, dc, t1, t2, t3, k_dl, k_dc)
                if n % TPB:
                    k_ec, ec_, f_ec = yield from r_ec.take()
                    yield from at(pe, t2, t3, t_ind)
                    for m in range(2):
                        t = pe.do(lambda e, m=m, bk=bk, dl=dl: e.matmul(
                            bk[:, 192 + 128 * m:320 + 128 * m], ind[:, 128 * m:128 * m + 128], dl[0:32, :],
                            start=True, stop=True), "ec_mm" if m else None, ns=mmr(128))
                    yield from exp_turn()
                    yield from at(act, t, *f_ec)
                    t = act.do(lambda e, bk=bk, ec_=ec_: e.activation(ec_[:, :], bk[:, 192:448], ACT.Exp), "ec",
                               ns=ac(256))
                    release(bk, t2, t3, t)
                    done[("ec", n)] = (k_ec, ec_, t)

        def p2r():
            for n in range(NT):
                yield from need(("cum", n))
                dl, t_hi, t_lo = done[("cum", n)]
                for j in range(2):
                    w = ()
                    if n:
                        yield from need(("D", n - 1, 2 * j), ("D", n - 1, 2 * j + 1))
                        w = (done[("D", n - 1, 2 * j)], done[("D", n - 1, 2 * j + 1)])
                    for r in range(2):
                        yield from at(sp, t_hi, t_lo, done["init"][0], *w)
                        t = sp.do(lambda e, dl=dl, j=j, r=r: e.dma_start(
                            RB[32 + r:33 + r, 1024 * j:1024 * j + 1024].rearrange("p (h t) -> p h t", h=8).bitcast(F),
                            dl[16 * r + 8 * j:16 * r + 8 * j + 8, :].bitcast(F)), f"cum_rows{j}", 16)
                    done[("rows", n, j)] = t

        def p2g(lane, lanes_):
            for s in range(lane, 4 * NT, lanes_):
                n, q = divmod(s, 4)
                g, i = divmod(n, GT)
                yield from need(("P2a", n), ("rows", n, q // 2), ("P1", g))
                if s >= lanes_:
                    yield from need(("g_start", s - 1))
                dl, _, t_hi, _, t_lo, k_dl, _ = done[("P2a", n)]
                t_rows = done[("rows", n, q // 2)]
                cols = slice(128 * i, 128 * i + 128)
                k_e, eb, f_e = yield from r_E.take()
                done[("g_start", s)] = True
                yield from at(pe, t_rows, t_hi, t_lo)
                bd = yield from bank()
                t_d = pe.do(lambda e, q=q, bd=bd, dl=dl: e.matmul(bd[:, :], dl[:, :],
                            RB[:, 512 * q:512 * q + 512], start=True, stop=True), "diff_mm", ns=mmr(512))
                done[("D", n, q)] = t_d
                if q == 3:
                    if n % TPB:
                        yield from need(("ec", n))
                    yield from need(("D", n, 0), ("D", n, 1), ("D", n, 2))
                    r_DL.free[k_dl] = tuple(done[("D", n, j)] for j in range(4))
                yield from at(pe, *done[("P1", g)])
                bg = yield from bank()
                for k, h in enumerate(heads(q)):
                    r0 = 64 * (h % 2)
                    t_g = pe.do(lambda e, k=k, h=h, r0=r0, bg=bg, cols=cols: e.matmul(
                        bg[:, 128 * k:128 * k + 128], Bc[r0:r0 + 64, h // 2, cols],
                        Cc[r0:r0 + 64, h // 2, cols], start=True, stop=True), "g_mm" if k == 3 else None, ns=mm(128))
                done[("G", n, q)] = t_g
                yield from exp_turn()
                yield from at(act, t_d, done["init"][1], *f_e)
                t_ex = act.do(lambda e, eb=eb, bd=bd: e.activation(
                    eb[:, :, :], bd[:, :].rearrange("p (h t) -> p h t", h=4), ACT.Exp), "decay_exp", ns=ac(512))
                release(bd, t_ex)
                yield from at(pool, t_ex)
                t_m = pool.do(lambda e, eb=eb: e.affine_select(
                    out=eb[:, :, :], in_=eb[:, :, :], compare_op=ALU.is_ge, fill=0.0, base=0,
                    pattern=[[0, 4], [1, 128]], channel_multiplier=-1), "causal", ns=600)
                yield from at(dve, t_m, t_g)
                t_e = dve.do(lambda e, eb=eb, bg=bg: e.tensor_tensor(
                    eb[:, :, :], bg[:, :].rearrange("p (h t) -> p h t", h=4), eb[:, :, :], ALU.mult), "ag", ns=ve(512))
                release(bg, t_e)
                done[("E", n, q)] = (k_e, eb, t_e)

        def p2i():
            for n in range(NT):
                g, i = divmod(n, GT)
                k_t, yt, f_t = yield from r_yT.take()
                if n % TPB == 0:
                    done[("C", n)] = None
                    done[("yd", n)] = (k_t, yt, f_t)
                    continue
                yield from need(("state", n - 1), ("P1", g), ("ec", n))
                s_old, t_s, _ = done[("state", n - 1)]
                k_ec, ec_, t_ec = done[("ec", n)]
                yield from at(pe, t_s, *done[("P1", g)])
                bi = yield from bank()
                for p in range(8):
                    t_in = pe.do(lambda e, p=p, bi=bi, s_old=s_old, i=i: e.matmul(
                        bi[32 * (p % 4):32 * (p % 4) + 32, 128 * (p // 4):128 * (p // 4) + 128], s_old[:, p, :],
                        Cc[:, p, 128 * i:128 * i + 128], start=True, stop=True, skip_group_check=True),
                        "inter_mm" if p == 7 else None, ns=mmc(128))
                done[("s_read", n - 1)] = done[("C", n)] = t_in
                yield from at(dve, t_in, t_ec, *f_t)
                t = dve.do(lambda e, yt=yt, bi=bi, ec_=ec_: e.tensor_tensor(yt[:, :], bi[:, 0:256], ec_[:, :], ALU.mult),
                           "y_dec", ns=ve(256))
                release(bi, t)
                done[("yd", n)] = (k_t, yt, (t,))
                yield from need(("P2s", n))
                r_ec.free[k_ec] = (t, *done[("P2s", n)][1:])

        def p2y():
            for n in range(NT):
                g, i = divmod(n, GT)
                x4 = n % (2 * GT)
                yield from need(("E", n, 0))
                yield from at(pe, done[("E", n, 0)][2], *done[("P1t", n)])
                by = yield from bank()
                for q in range(4):
                    yield from need(("E", n, q))
                    k_e, eb, t_e = done[("E", n, q)]
                    yield from at(pe, t_e)
                    for k, h in enumerate(heads(q)):
                        p, r = divmod(h, 2)
                        t = pe.do(lambda e, k=k, q=q, p=p, r=r, eb=eb, by=by, x4=x4: e.matmul(
                            by[32 * (p % 4):32 * (p % 4) + 32, 128 * (p // 4):128 * (p // 4) + 128],
                            Xt[:, x4, p, 16 * r:16 * r + 32], eb[:, k, :], start=q == 0, stop=r == 1,
                            skip_group_check=True), "y_mm" if k == 3 else None, ns=mmc(128))
                    r_E.free[k_e] = (t,)
                done[("P2y", n)] = (by, t)

        def p2s():
            t_st_read = None
            for n in range(NT):
                g, i = divmod(n, GT)
                if n % TPB == TPB - 1:
                    done[("P2s", n)] = ()
                    yield from need(("Bt", g))
                    k_bt, bt, t_bt = done[("Bt", g)][i]
                    r_Bt.free[k_bt] = (t_bt,)
                    yield from need(("s_read", n - 1))
                    r_St.free[done[("state", n - 1)][2]] = (done[("s_read", n - 1)],)
                    continue
                yield from need(("P2a", n))
                _, dc, _, t_dec, _, _, _ = done[("P2a", n)]
                cols = slice(128 * i, 128 * i + 128)
                k_xd, xd, f_xd = yield from r_Xd.take()
                yield from at(pool, t_dec, *done[("P1t", n)], *f_xd)
                t_xd = pool.do(lambda e, xd=xd, x4=n % (2 * GT), dc=dc: e.tensor_tensor(
                    by_head(xd[:, :]), Xt[:, x4, :, :].rearrange("p a (k c) -> p a k c", c=16)[:, :, 0:3:2, :],
                    per_head(dc[:, 0:16]), ALU.mult), "xd", ns=580)
                yield from need(("Bt", g))
                k_bt, bt, t_bt = done[("Bt", g)][i]
                yield from at(pe, t_xd, t_bt)
                bs = yield from bank()
                for p in range(8):
                    t_sm = pe.do(lambda e, p=p, bs=bs, bt=bt, xd=xd: e.matmul(
                        bs[32 * (p % 4):32 * (p % 4) + 32, 128 * (p // 4):128 * (p // 4) + 128],
                        xd[:, 32 * p:32 * p + 32], bt[:, 128 * p:128 * p + 128], start=True, stop=True,
                        skip_group_check=True), "state_mm" if p == 7 else None, ns=mmc(128))
                r_Xd.free[k_xd] = (t_sm,)
                r_Bt.free[k_bt] = (t_sm,)
                if n % TPB:
                    yield from need(("ec", n))
                    ec_, t_ec = done[("ec", n)][1:3]
                    yield from at(dve, t_sm, t_ec, t_st_read)
                    for m in range(2):
                        t_st = dve.do(lambda e, m=m, bs=bs, ec_=ec_: e.scalar_tensor_tensor(
                            out=ST[:, m, :], in0=ST[:, m, :], scalar=ec_[:, 128 * m + 127:128 * m + 128],
                            in1=bs[:, 128 * m:128 * m + 128], op0=ALU.mult, op1=ALU.add), "state", ns=ve(128))
                else:
                    yield from at(dve, t_sm, t_st_read)
                    t_st = dve.do(lambda e, bs=bs: e.tensor_copy(
                        ST[:, :, :], bs[:, 0:256].rearrange("p (a b) -> p a b", a=2)), "state", ns=ve(256))
                release(bs, t_st)
                yield from at(pe, t_st, t_cst)
                bs = yield from bank()
                for m in range(2):
                    t_st_read = pe.do(lambda e, m=m, bs=bs: e.transpose(bs[:, 128 * m:128 * m + 128], ST[:, m, :],
                                      ident[:, :]), "sT_mm" if m else None, ns=100)
                k_s, s_new, f_s = yield from r_St.take()
                yield from at(act, t_st_read, t_s0, *f_s)
                for h2 in range(2):
                    r = slice(64 * h2, 64 * h2 + 64)
                    c = slice(16 * h2, 16 * h2 + 16)
                    t_s = act.do(lambda e, r=r, c=c, bs=bs, s_new=s_new: e.copy(
                        s_new[r, :, c], bs[r, 0:256].rearrange("p (a c) -> p a c", c=32)[:, :, c]), "state_T", ns=158)
                release(bs, t_s)
                done[("state", n)] = (s_new, t_s, k_s)
                done[("P2s", n)] = (t_xd, t_st)
                if n % TPB:
                    yield from need(("s_read", n - 1))
                    r_St.free[done[("state", n - 1)][2]] = (done[("s_read", n - 1)],)

        def layernorm(t_mm, bk, resid, w_res, r, w_r, mark):
            k, s_, f_s = yield from r_st.take()
            yield from at(dve, t_mm, *w_res, *w_r)
            t0 = dve.do(lambda e: e.tensor_tensor(r, bk[:, 0:256], resid, ALU.add), "ln_add", ns=ve(256))
            release(bk, t0)
            yield from at(dve, t0, *f_s)
            t1 = dve.do(lambda e: e.bn_stats(s_[:, 0:6], r), "ln_stats", ns=ve(256))
            yield from at(dve, t1)
            t2 = dve.do(lambda e: e.bn_aggr(s_[:, 6:8], s_[:, 0:6]), "ln_aggr", ns=80)
            yield from at(pool, t2, t_cst)
            t3 = pool.do(lambda e: e.tensor_scalar(s_[:, 8:9], s_[:, 7:8], EPS, None, ALU.add), "ln_eps", ns=180)
            yield from at(pool, t3)
            t4 = pool.do(lambda e: e.tensor_tensor(s_[:, 9:10], s_[:, 8:9], mhalf[:, 0:1], ALU.pow), "ln_rstd", ns=470)
            yield from at(dve, t4)
            t5 = dve.do(lambda e: e.tensor_scalar(r, r, s_[:, 6:7], s_[:, 9:10], ALU.subtract, ALU.mult), mark,
                        ns=ve(256, True) + 120)
            r_st.free[k] = (t5,)
            return t0, t5

        def transpose2(src, w_src, dst, w_dst, mark):
            yield from at(pe, t_cst, *w_src)
            bk = yield from bank()
            for k in range(2):
                t = pe.do(lambda e, k=k: e.transpose(bk[:, 128 * k:128 * k + 128], src[:, 128 * k:128 * k + 128],
                          ident[:, :]), mark + "_pe" if k else None, ns=100)
            yield from at(act, t, *w_dst)
            t2 = act.do(lambda e: e.copy(dst, bk[:, 0:256].rearrange("p (a b) -> p a b", a=2)), mark, ns=ac(256))
            release(bk, t2)
            return t, t2

        t_wo, t_wb = Token("ld_w", 64, 30e3), Token("ld_b", 80, 30e3)

        def p2x():
            for n in range(NT):
                k_xr, x_, f_x = yield from r_xr.take()
                yield from at(sp, *f_x)
                t_x = load(x_[:, :], a["x"][128 * n:128 * n + 128, :], f"ld_x{k_xr}")
                yield from at(pool, t_x, t_wb)
                t_x = pool.do(lambda e, x_=x_: e.tensor_tensor(x_[:, :], x_[:, :], bo[:, :], ALU.add), "x_bias", ns=690)
                done[("xr", n)] = (x_, t_x, k_xr)

        def p2c():
            for n in range(NT):
                g, i = divmod(n, GT)
                yield from need(("P2y", n), ("P2s", n))
                by, t_y = done[("P2y", n)]
                k_dc = done[("P2a", n)][6]
                yield from need(("gate", g), ("yd", n))
                k_t, yt, w_y = done[("yd", n)]
                gate = gT[:, g % 2, :, 128 * i:128 * i + 128]
                yv = yt[:, :].rearrange("p (a b) -> p a b", a=2)
                yield from at(dve, t_y, done[("gate", g)], *w_y)
                if n % TPB == 0:
                    t = dve.do(lambda e, yv=yv, by=by, gate=gate: e.tensor_tensor(
                        yv, by[:, 0:256].rearrange("p (a b) -> p a b", a=2), gate, ALU.mult), "y_gate", ns=ve(256))
                    release(by, t)
                else:
                    t = dve.do(lambda e, yt=yt, by=by: e.tensor_tensor(yt[:, :], by[:, 0:256], yt[:, :], ALU.add),
                               "y_sum", ns=ve(256))
                    release(by, t)
                    yield from at(dve, t)
                    t = dve.do(lambda e, yv=yv, gate=gate: e.tensor_tensor(yv, yv, gate, ALU.mult), "y_gate",
                               ns=ve(256))
                t_s = done[("P2s", n)]
                r_dec.free[k_dc] = (done[("P2a", n)][3], *t_s[0:1])
                done[("P2", n)] = (t, t_y, *t_s)
                t_t = t
                yield from at(pe, t_t, t_wo)
                bk = yield from bank()
                for k in range(2):
                    t = pe.do(lambda e, k=k, bk=bk, yt=yt: e.matmul(bk[:, 0:256], yt[:, 128 * k:128 * k + 128], wout[:, k, :],
                              start=k == 0, stop=k == 1), "wout_mm" if k else None, ns=mm(256))
                r_yT.free[k_t] = (t,)
                yield from need(("xr", n))
                x_, t_x, k_xr = done[("xr", n)]
                if n >= X1N:
                    yield from need(("x1free", n - X1N))
                w = (done[("x1free", n - X1N)],) if n >= X1N else ()
                t0, t5 = yield from layernorm(t, bk, x_[:, :], (t_x,), x1[:, n % X1N, :], w, "ln1")
                r_xr.free[k_xr] = (t0,)
                done[("x1", n)] = t5

        def p3q():
            for g in range(NG):
                w_t = (done[("q", g - 1)][0],) if g else ()
                for i in range(GT):
                    n = GT * g + i
                    yield from need(("x1", n))
                    x = x1[:, n % X1N, :]
                    t_pe, t_t = yield from transpose2(x, (done[("x1", n)],), tT[:, :, 128 * i:128 * i + 128], w_t, "x1T")
                    yield from at(pool, t_pe, t_wb)
                    done[("x1b", n)] = pool.do(lambda e, x=x: e.tensor_tensor(x, x, bp[:, :], ALU.add), "x1b", ns=690)
                w_q = (done[("q", g - 1)][1],) if g else ()
                for m in range(2):
                    yield from at(pe, t_t, t_wo)
                    bk = yield from bank()
                    for k in range(2):
                        t = pe.do(lambda e, bk=bk, m=m, k=k: e.matmul(bk[:, 0:GW], qw[:, k, 128 * m:128 * m + 128],
                                  tT[:, k, :], start=k == 0, stop=k == 1), "q_mm" if k else None, ns=mm(GW))
                    yield from at(act, t, t_wb, *w_q)
                    t1 = act.do(lambda e, bk=bk, m=m: e.activation(qhi[:, m, :].bitcast(R), bk[:, 0:GW], ACT.Identity,
                                bias=qbc[:, m:m + 1]), "q_hi", ns=ac(GW) + 90)
                    yield from at(dve, t1, *w_q)
                    t2 = dve.do(lambda e, bk=bk, m=m: e.scalar_tensor_tensor(
                        out=qf[:, m, :].bitcast(R), in0=bk[:, 0:GW], scalar=qbc[:, m:m + 1], in1=qhi[:, m, :],
                        op0=ALU.add, op1=ALU.subtract), "q_lo", ns=ve(GW) + 60)
                    release(bk, t1, t2)
                if g:
                    yield from need(("P3pe", g - 1))
                w = [done[("P3pe", g - 1)]] if g else [t_q1]
                yield from at(sp, t2, *w)
                done[("q", g)] = (t, (yield from stack(qhi, qf, qst, t1, t2, w, "q_stack")))

        def p3a(lane, lanes_):
            yield from need("kv")
            t_ks, t_vs, t_mr = done["kv"]
            for n in range(lane, NT, lanes_):
                g, i = divmod(n, GT)
                b = n // TPB
                yield from need(("q", g))
                if n:
                    yield from need(("a_start", n - 1))
                k_m, m_, f_m = yield from r_mx.take()
                k_p, pb, f_p = yield from r_P.take()
                done[("a_start", n)] = True
                for j in range(3):
                    n0, n1 = 3 * j, min(3 * j + 3, 8)
                    w = (n1 - n0) * 2
                    yield from at(pe, done[("q", g)][1], t_ks, t_mr)
                    bk = yield from bank()
                    for p in range(n0, n1):
                        t = pe.do(lambda e, p=p, n0=n0, bk=bk, i=i, b=b: e.matmul(
                            bk[:, 2 * S * (p - n0):2 * S * (p - n0 + 1)], qst[0:97, p, 128 * i:128 * i + 128],
                            kst[0:97, b, p, :], start=True, stop=True), "s_mm" if p == n1 - 1 else None, ns=mmr(2 * S))
                    v = bk[:, 0:w * S].rearrange("p (h s) -> p h s", s=S)
                    yield from at(dve, t, *f_m)
                    t1 = dve.do(lambda e, v=v, m_=m_, n0=n0, w=w: e.tensor_reduce(m_[:, 2 * n0:2 * n0 + w], v, AX, ALU.max),
                                "s_max", ns=ve(S * w))
                    yield from at(dve, t1, *f_p)
                    t2 = dve.do(lambda e, v=v, m_=m_, n0=n0, w=w, pb=pb: e.tensor_tensor(
                        pb[:, 2 * S * n0:2 * S * n0 + w * S].rearrange("p (h s) -> p h s", s=S), v,
                        m_[:, 2 * n0:2 * n0 + w].unsqueeze(2).to_broadcast([128, w, S]), ALU.subtract),
                        "s_sub", ns=ve(S * w))
                    release(bk, t2)
                r_mx.free[k_m] = (t2,)
                done[("S", n)] = t
                if i == GT - 1:
                    yield from need(*((("S", m) for m in range(GT * g, n))))
                    done[("P3pe", g)] = t
                yield from exp_turn()
                yield from at(act, t2)
                t3 = act.do(lambda e, pb=pb: e.activation(pb[:, :], pb[:, :], ACT.Exp, scale=SCALE), "p_exp", ns=ac(HS))
                k_r, rc_, f_rc = yield from r_rc.take()
                pv = pb[:, :].rearrange("p (h s) -> p h s", s=S)
                yield from at(dve, t3, *f_rc)
                t4 = dve.do(lambda e, rc_=rc_, pv=pv: e.tensor_reduce(rc_[:, :], pv, AX, ALU.add), "p_sum", ns=ve(HS))
                yield from at(dve, t4)
                t4 = dve.do(lambda e, rc_=rc_: e.reciprocal(rc_[:, :], rc_[:, :]), "p_rcp", ns=170)
                for j in range(4):
                    yield from at(pool, t4)
                    t5 = pool.do(lambda e, pv=pv[:, 4 * j:4 * j + 4, :], rc_=rc_[:, 4 * j:4 * j + 4]: e.tensor_tensor(
                        pv, pv, rc_.unsqueeze(2).to_broadcast([128, 4, S]), ALU.mult), "p_norm", ns=661)
                r_rc.free[k_r] = (t5,)
                done[("P", n)] = (pb, t5, k_p)

        def p3b():
            for n in range(NT):
                b = n // TPB
                yield from need(("P", n))
                pb, t3, k_p = done[("P", n)]
                k_pt, pt, f_pt = yield from r_PT.take()
                tps = []
                for j in range(3):
                    m0, m1 = 4 * j, min(4 * j + 4, NBLK)
                    yield from at(pe, t3, t_cst)
                    bk = yield from bank()
                    for m in range(m0, m1):
                        w = blk_rows(m)
                        t = pe.do(lambda e, m=m, m0=m0, w=w, bk=bk, pb=pb: e.transpose(
                            bk[0:w, 128 * (m - m0):128 * (m - m0) + 128], pb[:, 128 * m:128 * m + w], ident[:, :]),
                            "pT_mm" if m == m1 - 1 else None, ns=100)
                    if j < 2:
                        q = act if j == 0 else dve
                        yield from at(q, t, *f_pt)
                        t4 = q.do(lambda e, m0=m0, m1=m1, bk=bk, pt=pt, j=j: (e.tensor_copy if j else e.copy)(
                            pt[:, m0:m1, :], bk[:, :].rearrange("p (a b) -> p a b", b=128)), "pT_v" if j else "pT", ns=598 if j else 478)
                    else:
                        w = blk_rows(9)
                        yield from at(act, t, *f_pt)
                        act.do(lambda e, bk=bk, pt=pt: e.copy(pt[:, 8, :], bk[:, 0:128]), "pT", ns=158)
                        t4 = act.do(lambda e, bk=bk, pt=pt, w=w: e.copy(pt[0:w, 9, :], bk[0:w, 128:256]), "pT", ns=158)
                    tps.append(t4)
                    release(bk, t4)
                r_P.free[k_p] = (t,)
                yield from at(pe, *tps, done["kv"][1])
                bo_ = yield from bank()
                for j, (p, m, first, last_) in enumerate(PV):
                    w = blk_rows(m)
                    t = pe.do(lambda e, j=j, p=p, m=m, w=w, first=first, last_=last_, bo_=bo_, pt=pt, b=b: e.matmul(
                        bo_[32 * (p % 4):32 * (p % 4) + 32, 128 * (p // 4):128 * (p // 4) + 128],
                        vb[0:w, b, j, :], pt[0:w, m, :], start=first and p < 4, stop=last_, skip_group_check=True),
                        "pv_mm" if j == len(PV) - 1 else None, ns=mmc(128))
                r_PT.free[k_pt] = (t,)
                k_t, ot, f_t = yield from r_oT.take()
                yield from at(act, t, *f_t)
                t2 = act.do(lambda e, bo_=bo_, ot=ot: e.copy(
                    ot[:, :, :], bo_[:, 0:256].rearrange("p (a b) -> p a b", a=2)), "oT", ns=ac(256))
                release(bo_, t2)
                done[("O", n)] = (ot, t2, k_t)

        def p3c():
            for n in range(NT):
                yield from need(("O", n))
                ot, t_t, k_t = done[("O", n)]
                yield from at(pe, t_t, t_wo)
                bk = yield from bank()
                for k in range(2):
                    t = pe.do(lambda e, k=k, bk=bk, ot=ot: e.matmul(bk[:, 0:256], ot[:, k, :], pw[:, k, :],
                              start=k == 0, stop=k == 1), "proj_mm" if k else None, ns=mm(256))
                r_oT.free[k_t] = (t,)
                if n >= X2N:
                    yield from need(("x2free", n - X2N))
                w = (done[("x2free", n - X2N)],) if n >= X2N else (done["kv"][1],)
                t0, t5 = yield from layernorm(t, bk, x1[:, n % X1N, :], (done[("x1b", n)],), x2[:, n % X2N, :], w, "ln2")
                done[("x1free", n)] = t0
                done[("x2", n)] = t5

        def p4a():
            t_f1 = None
            yield from need("kv")
            for g in range(NF):
                for i in range(FT):
                    n = FT * g + i
                    yield from need(("x2", n))
                    x = x2[:, n % X2N, :]
                    cols = slice(128 * i, 128 * i + 128)
                    yield from at(pe, t_cst, done[("x2", n)])
                    bk = yield from bank()
                    for k in range(2):
                        t_pe = pe.do(lambda e, k=k, x=x, bk=bk: e.transpose(
                            bk[:, 128 * k:128 * k + 128], x[:, 128 * k:128 * k + 128], ident[:, :]),
                            "x2T_pe" if k else None, ns=100)
                    v = bk[:, 0:256].rearrange("p (a b) -> p a b", a=2)
                    yield from at(act, t_pe, t_f1)
                    t = act.do(lambda e, v=v, cols=cols: e.copy(uh[:, :, cols], v), "u_hi", ns=ac(256))
                    yield from at(dve, t, t_f1)
                    t_t = dve.do(lambda e, v=v, cols=cols: e.tensor_tensor(
                        ul[:, :, cols], v, uh[:, :, cols].bitcast(F), ALU.subtract), "u_lo", ns=ve(256))
                    release(bk, t_t)
                    yield from at(pool, t_pe, t_wb)
                    done[("x2b", n)] = pool.do(lambda e, x=x: e.tensor_tensor(x, x, b2[:, :], ALU.add), "x2b", ns=690)
                yield from need("w1")
                w = (done["kv"][1], done["w1"])
                if g:
                    yield from need(("F2", FT * g - 1))
                    w = (done[("F2", FT * g - 1)],)
                t_r = []
                for m in range(8):
                    yield from at(pe, t_t, t_wo)
                    bk = yield from bank()
                    for k, (wm, um) in enumerate(((w1h, uh), (w1h, uh), (w1l, uh), (w1l, uh), (w1h, ul), (w1h, ul))):
                        t_f1 = pe.do(lambda e, bk=bk, m=m, k=k, wm=wm, um=um: e.matmul(
                            bk[:, 0:128 * FT], wm[:, k % 2, 128 * m:128 * m + 128], um[:, k % 2, :],
                            start=k == 0, stop=k == 5), "ffn1_mm" if k == 5 else None, ns=mmr(128 * FT))
                    yield from at(act, t_f1, t_wb, *w)
                    t = act.do(lambda e, bk=bk, m=m: e.activation(hT[:, m, :], bk[:, 0:128 * FT], ACT.Relu,
                               bias=b1c[:, m:m + 1]), "relu", ns=ac(128 * FT) + 90)
                    release(bk, t)
                    t_r.append(t)
                done[("h", g)] = t_r

        def p4b():
            for n in range(NT):
                g, i = divmod(n, FT)
                yield from need(("h", g))
                k_r, r, f_r = yield from r_res.take()
                for m in range(8):
                    if m % 4 == 0:
                        yield from at(pe, done[("h", g)][m + 3])
                    if m == 0:
                        bk = yield from bank()
                    t = pe.do(lambda e, bk=bk, m=m, i=i: e.matmul(bk[:, 0:256], hT[:, m, 128 * i:128 * i + 128],
                              w2[:, m, :], start=m == 0, stop=m == 7), "ffn2_mm" if m == 7 else None, ns=mm(256))
                done[("F2", n)] = t
                t0, t5 = yield from layernorm(t, bk, x2[:, n % X2N, :], (done[("x2b", n)],), r[:, :], f_r, "ln3")
                done[("x2free", n)] = t0
                yield from at(sp, t5)
                t = sp.do(lambda e, n=n, r=r: e.dma_start(out[128 * n:128 * n + 128, :], r[:, :]), f"store{k_r}", 16)
                r_res.free[k_r] = (t,)
                stores.append(t)

        stores = []
        interleave([p_load(), p_init(), p2g(0, 3), p2g(1, 3), p2g(2, 3), p1(), p2c(), p2i(), p2y(), p2s(), p2r(), p2a(), p2x(),
                    p_weights(), p_kv(), p3q(), p3c(), p3b(), p3a(0, 2), p3a(1, 2), p4a(), p4b()], (pe, act, dve, pool, sp))
        sp.wait(*stores)

        block = ctx.enter_context(nc.Block())

        @block.sync
        def _(eng):
            sp.run(eng)

        @block.tensor
        def _(eng):
            pe.run(eng)

        @block.vector
        def _(eng):
            dve.run(eng)

        @block.scalar
        def _(eng):
            act.run(eng)

        @block.gpsimd
        def _(eng):
            pool.run(eng)


def stacked_weights(W_XBC, b_XBC, W_logA, b_logA, W_gate):
    w = np.zeros((KX, WCOLS), W_XBC.dtype)
    g = np.zeros((32, 256), W_gate.dtype)

    def put(col, h, rows, bias):
        r = 16 * (h % 2)
        for k in range(3):
            w[32 * k + r:32 * k + r + 16, col:col + rows.shape[0]] = rows.T
        w[96:98, col:col + rows.shape[0]] = bias

    for h in range(H):
        p, h2 = divmod(h, 2)
        put(WT * p + 64 * h2, h, W_XBC[h, 16:80], b_XBC[h, 16:80])
        put(WT * p + 128 + 16 * h2, h, W_XBC[h, 0:16], b_XBC[h, 0:16])
        put(WT * p + 160 + h2, h, W_logA[h], b_logA[h])
        put(WC + 128 * p + 64 * h2, h, W_XBC[h, 80:144], b_XBC[h, 80:144])
        g[16 * h2:16 * h2 + 16, 32 * p + 16 * h2:32 * p + 16 * h2 + 16] = W_gate[h].T
    return w, g


def kernel(x, ctx_1024, mask_BxS2_bk0, L0_attn_W_logA, L0_attn_b_logA, L0_attn_W_XBC, L0_attn_b_XBC,
           L0_attn_W_gate, L0_attn_b_gate, L0_attn_W_out, L0_attn_b_out, L0_xattn_q_w, L0_xattn_q_b,
           L0_xattn_kv_w, L0_xattn_kv_b, L0_xattn_proj_w, L0_xattn_proj_b, L0_ffn_W1, L0_ffn_b1,
           L0_ffn_W2, L0_ffn_b2):
    import concourse.bacc as _bacc
    from concourse.bass_utils import run_bass_kernel_spmd as _run

    f = np.float32
    A = np.asarray

    def kmajor(w):
        w = A(w)
        return w.reshape(-1, 128, w.shape[1]).transpose(1, 0, 2)

    def col(v):
        return A(v).reshape(-1, 128).T

    def rows(v, n):
        return np.broadcast_to(A(v), (n, A(v).shape[0]))

    xf = A(x).reshape(B * T, D)
    kvb = A(L0_xattn_kv_b)
    mask = A(mask_BxS2_bk0)
    idx = np.arange(128)
    tri = (idx[:, None] <= idx[None, :]).astype(f)
    dl = np.zeros((34, 128), f)
    dl[32:34] = 1.0
    rb = np.zeros((34, 16, 128), f)
    for h in range(16):
        rb[h, h] = -1.0
        rb[16 + h, h] = -1.0
    ind = np.zeros((2, 2, 8, 8, 2, 16), f)
    for r in range(2):
        for m in range(8):
            ind[:, r, m, m, r] = 1.0
    negm = np.zeros((128, 1), f)
    negm[64:97] = -1.0
    negl = np.zeros((32, 1), f)
    negl[16:32] = -1.0
    wst, wg = stacked_weights(A(L0_attn_W_XBC), A(L0_attn_b_XBC), A(L0_attn_W_logA), A(L0_attn_b_logA),
                              A(L0_attn_W_gate))
    arrays = {
        "x": xf,
        "x3": np.tile(xf.T.reshape(8, 32, B * T).transpose(1, 0, 2), (3, 1, 1)),
        "wst": wst, "wg": wg,
        "negm": negm, "negl": negl, "ind": ind.reshape(32, 256), "dl": dl, "rb": rb.reshape(34, 2048),
        "ident": np.eye(128, dtype=f), "tri": tri,
        "sup": (idx[:, None] > idx[None, :]).astype(f),
        "mhalf": np.full((128, 1), -0.5, f),
        "wout": kmajor(A(L0_attn_W_out).T), "pw": kmajor(L0_xattn_proj_w), "qw": kmajor(L0_xattn_q_w),
        "kvw": kmajor(L0_xattn_kv_w), "w1": kmajor(L0_ffn_W1), "w2": kmajor(L0_ffn_W2),
        "b1": col(L0_ffn_b1), "qb": col(L0_xattn_q_b), "kb": col(kvb[0:256]), "gb": col(L0_attn_b_gate),
        "bo": rows(L0_attn_b_out, 128), "bp": rows(L0_xattn_proj_b, 128), "b2": rows(L0_ffn_b2, 128),
        "bv": rows(kvb[256:512], S),
        "ctxT": A(ctx_1024).reshape(B * S, D).T.reshape(2, 128, B * S).transpose(1, 0, 2),
        "mcol": mask.T, "mrow": mask.reshape(1, B * S),
    }
    nc = _bacc.Bacc("TRN2", target_bir_lowering=False, num_devices=1)
    maps, aps = {}, {}
    for name, v in arrays.items():
        v = np.ascontiguousarray(v)
        maps[f"in_{name}"] = v
        aps[name] = nc.dram_tensor(f"in_{name}", v.shape, mybir.dt.from_np(v.dtype), kind="ExternalInput").ap()
    out = nc.dram_tensor("out_0", (B * T, D), F, kind="ExternalOutput").ap()
    build(nc, aps, out)
    r = _run(nc, [maps], core_ids=[0])
    return r.results[0]["out_0"].reshape(B, T, D)
```
